# Optimizing a Trainium2 kernel written in Bass

```python
import numpy as np
import jax
import jax.numpy as jnp

def _softmax(x, axis=-1):
    return jax.nn.softmax(x, axis=axis)

def _gelu(x):
    return jax.nn.gelu(x, approximate=True)

def _silu(x):
    return jax.nn.silu(x)

def _sigmoid(x):
    return jax.nn.sigmoid(x)

def _layernorm(x, axis=-1, eps=1e-05):
    m = jnp.mean(x, axis=axis, keepdims=True)
    v = jnp.var(x, axis=axis, keepdims=True)
    return (x - m) / jnp.sqrt(v + eps)

def _scatter_add(tgt, idx, src, axis=0):
    return tgt.at[idx].add(src)

def _segment_sum(src, seg, n):
    return jax.ops.segment_sum(src, seg, n)
kernel_name = 'mk_sandwich_d1_jaxref_r8_49bcbe'

def setup_inputs(seed: int=0):
    np.random.seed(seed)
    _w = jnp.asarray

    def _L0_attn_setup():
        import jax, jax.numpy as jnp
        import numpy as np
        EMB = 128
        HEADS = 16
        EPS = 1e-05

        def layer_norm(x):
            mu = jnp.mean(x, axis=-1, keepdims=True)
            var = jnp.var(x, axis=-1, keepdims=True)
            return (x - mu) / jnp.sqrt(var + EPS)

        def pattention(x, K, V):
            scale = EMB ** (-0.5)
            a = jax.nn.softmax(scale * jnp.einsum('btc,nc->btn', x, K), axis=-1)
            return jnp.einsum('btn,nc->btc', a, V)

        def causal_sdpa(q, k, v):
            T = q.shape[2]
            d = q.shape[-1]
            scores = jnp.einsum('bhqd,bhkd->bhqk', q, k) / jnp.sqrt(jnp.asarray(d, q.dtype))
            mask = jnp.tril(jnp.ones((T, T), dtype=bool))
            scores = jnp.where(mask, scores, jnp.asarray(-jnp.inf, q.dtype))
            attn = jax.nn.softmax(scores, axis=-1)
            return jnp.einsum('bhqk,bhkd->bhqd', attn, v)
        key = jax.random.key(seed)
        ks = jax.random.split(key, 11)
        B, T, C = (2, 256, EMB)
        N = 256 // 2
        inp = {'x': jax.random.normal(ks[0], (B, T, C), dtype=jnp.float32)}
        names = ['qK', 'qV', 'kK', 'kV', 'vK', 'vV', 'pK', 'pV']
        for i, nm in enumerate(names):
            inp[nm] = jax.random.normal(ks[1 + i], (N, C), dtype=jnp.float32)
        inp['fK'] = jax.random.normal(ks[9], (4 * N, C), dtype=jnp.float32)
        inp['fV'] = jax.random.normal(ks[10], (4 * N, C), dtype=jnp.float32)
        return inp
    _L0_attn_in = _L0_attn_setup()

    def _L0_ffn_setup():
        import jax, jax.numpy as jnp
        import numpy as np
        EPS = 1e-05

        def _quantize(W):
            gamma = jnp.mean(jnp.abs(W))
            return jnp.clip(jnp.round(W / (gamma + EPS)), -1.0, 1.0)
        key = jax.random.key(seed)
        k_x, k_w1, k_b1, k_w2, k_b2 = jax.random.split(key, 5)
        n_embd = 128
        d_ff = 4 * n_embd
        B, S = (4, 512)
        bound1 = 1.0 / np.sqrt(n_embd)
        bound2 = 1.0 / np.sqrt(d_ff)
        x = jax.random.normal(k_x, (B, S, n_embd), dtype=jnp.float32)
        W1 = jax.random.uniform(k_w1, (d_ff, n_embd), jnp.float32, -bound1, bound1)
        b1 = jax.random.uniform(k_b1, (d_ff,), jnp.float32, -bound1, bound1)
        W2 = jax.random.uniform(k_w2, (n_embd, d_ff), jnp.float32, -bound2, bound2)
        b2 = jax.random.uniform(k_b2, (n_embd,), jnp.float32, -bound2, bound2)
        return {'x': x, 'W1': W1, 'b1': b1, 'W2': W2, 'b2': b2}
    _L0_ffn_in = _L0_ffn_setup()
    _d = {'L0_attn_x': _L0_attn_in['x'], 'L0_attn_qK': _L0_attn_in['qK'], 'L0_attn_qV': _L0_attn_in['qV'], 'L0_attn_kK': _L0_attn_in['kK'], 'L0_attn_kV': _L0_attn_in['kV'], 'L0_attn_vK': _L0_attn_in['vK'], 'L0_attn_vV': _L0_attn_in['vV'], 'L0_attn_pK': _L0_attn_in['pK'], 'L0_attn_pV': _L0_attn_in['pV'], 'L0_attn_fK': _L0_attn_in['fK'], 'L0_attn_fV': _L0_attn_in['fV'], 'L0_ffn_W1': _L0_ffn_in['W1'], 'L0_ffn_b1': _L0_ffn_in['b1'], 'L0_ffn_W2': _L0_ffn_in['W2'], 'L0_ffn_b2': _L0_ffn_in['b2']}
    _x0 = _d['L0_attn_x']
    _d['L0_attn_x'] = jax.random.normal(jax.random.fold_in(jax.random.key(seed), 1), (16, 256, 128), dtype=_x0.dtype)
    del _x0
    return _d

def reference(L0_attn_x, L0_attn_qK, L0_attn_qV, L0_attn_kK, L0_attn_kV, L0_attn_vK, L0_attn_vV, L0_attn_pK, L0_attn_pV, L0_attn_fK, L0_attn_fV, L0_ffn_W1, L0_ffn_b1, L0_ffn_W2, L0_ffn_b2):

    def _L0_attn_ref(x, qK, qV, kK, kV, vK, vV, pK, pV, fK, fV):
        import jax, jax.numpy as jnp
        import numpy as np
        EMB = 128
        HEADS = 16
        EPS = 1e-05

        def layer_norm(x):
            mu = jnp.mean(x, axis=-1, keepdims=True)
            var = jnp.var(x, axis=-1, keepdims=True)
            return (x - mu) / jnp.sqrt(var + EPS)

        def pattention(x, K, V):
            scale = EMB ** (-0.5)
            a = jax.nn.softmax(scale * jnp.einsum('btc,nc->btn', x, K), axis=-1)
            return jnp.einsum('btn,nc->btc', a, V)

        def causal_sdpa(q, k, v):
            T = q.shape[2]
            d = q.shape[-1]
            scores = jnp.einsum('bhqd,bhkd->bhqk', q, k) / jnp.sqrt(jnp.asarray(d, q.dtype))
            mask = jnp.tril(jnp.ones((T, T), dtype=bool))
            scores = jnp.where(mask, scores, jnp.asarray(-jnp.inf, q.dtype))
            attn = jax.nn.softmax(scores, axis=-1)
            return jnp.einsum('bhqk,bhkd->bhqd', attn, v)
        B, T, C = x.shape
        H = HEADS
        D = C // H
        x_in = x
        h = layer_norm(x)
        k = pattention(h, kK, kV)
        q = pattention(h, qK, qV)
        v = pattention(h, vK, vV)
        to_heads = lambda t: t.reshape(B, T, H, D).transpose(0, 2, 1, 3)
        o = causal_sdpa(to_heads(q), to_heads(k), to_heads(v))
        o = o.transpose(0, 2, 1, 3).reshape(B, T, C)
        o = pattention(o, pK, pV)
        x = o + x_in
        x_inter = x
        x = pattention(layer_norm(x), fK, fV)
        return x + x_inter

    def _L0_ffn_ref(x, W1, b1, W2, b2):
        import jax, jax.numpy as jnp
        import numpy as np
        EPS = 1e-05

        def _quantize(W):
            gamma = jnp.mean(jnp.abs(W))
            return jnp.clip(jnp.round(W / (gamma + EPS)), -1.0, 1.0)
        Wq1 = _quantize(W1)
        Wq2 = _quantize(W2)
        h = jax.nn.relu(jnp.einsum('bsd,fd->bsf', x, Wq1) + b1)
        out = jnp.einsum('bsf,df->bsd', h, Wq2) + b2
        return out
    x = L0_attn_x
    x = x + _layernorm(_L0_attn_ref(_layernorm(x, axis=-1), L0_attn_qK, L0_attn_qV, L0_attn_kK, L0_attn_kV, L0_attn_vK, L0_attn_vV, L0_attn_pK, L0_attn_pV, L0_attn_fK, L0_attn_fV), axis=-1)
    x = x + _layernorm(_L0_ffn_ref(_layernorm(x, axis=-1), L0_ffn_W1, L0_ffn_b1, L0_ffn_W2, L0_ffn_b2), axis=-1)
    return x

_drawn_inputs = setup_inputs


def setup_inputs(seed=0):
    import zlib

    import numpy as np

    out = dict(_drawn_inputs(seed))
    spreads = {}
    factors = {'L0_attn_qK': 8.0,
     'L0_attn_qV': 8.0,
     'L0_attn_kK': 8.0,
     'L0_attn_kV': 8.0,
     'L0_attn_vK': 8.0,
     'L0_attn_vV': 8.0,
     'L0_attn_pK': 8.0,
     'L0_ffn_b1': 22.348,
     'L0_ffn_b2': 64.0}
    for name, (base, spread) in spreads.items():
        noise = np.random.default_rng([zlib.crc32(name.encode()), seed]).standard_normal(out[name].shape)
        drawn = base * np.exp(spread * noise) if base else spread * noise
        out[name] = jnp.asarray(drawn.astype(out[name].dtype))
    for name, factor in factors.items():
        out[name] = (out[name] * factor).astype(out[name].dtype)
    return out
```

```python
from contextlib import ExitStack

import concourse.bass as bass
from concourse import mybir

F32 = mybir.dt.float32
F32R = mybir.dt.float32r
BF16 = mybir.dt.bfloat16
ALU = mybir.AluOpType
ACT = mybir.ActivationFunctionType
AX = mybir.AxisListType

P = 128
EPS = 1e-5
MASKED = -1e30
TICKS = 32


class Sequence:

    def __init__(self, number, parity):
        self.number, self.parity = number, parity

    def has_before(self, n):
        return not isinstance(self.number, int) or self.number >= n

    def dmas(self, each, back=0):
        return self.number * (16 * each) + 16 * each * (1 - back)

    def dmas_of_parity(self, back=0):
        return (self.number - self.parity) * 8 + 16 * (1 - back // 2)


class Track:

    def __init__(self, sem, names):
        assert len(names) <= TICKS and len(set(names)) == len(names)
        self.sem, self.names = sem, list(names)

    def done(self, name):
        last = name == self.names[-1]
        return self.sem, TICKS - len(self.names) + 1 if last else 1

    def at(self, seq, name, back=0):
        k = self.names.index(name)
        rise = TICKS if k == len(self.names) - 1 else k + 1
        return self.sem, seq.number * TICKS + (rise - back * TICKS)


def build_block(nc, x, qK, qV, kK, kV, vK, vV, pK, pV, fK, fV, W1, b1, W2, b2, out):
    B, T, C = x.shape
    NP = qK.shape[0]
    NF = fK.shape[0]
    FF = W1.shape[0]
    H = 16
    D = C // H
    NT = T // P
    G = 4
    FC, KC = FF // P, NF // P
    ROWS = 3 * G * D
    SCALE = float(C) ** -0.5
    STAGES = 5
    assert (C, NP, NT, H, D, FC, KC) == (P, P, 2, 16, 8, 4, 4)

    with ExitStack() as ctx:
        def sb(name, shape, dt=F32):
            return ctx.enter_context(nc.sbuf_tensor(name, shape, dt))

        def bank(name):
            return ctx.enter_context(nc.psum_tensor(name, [P, 512], F32))

        def sem(name):
            return ctx.enter_context(nc.semaphore(name))

        def track(name, names):
            return Track(sem(name), names)

        ident = sb("ident", [P, P])
        ident_bf = sb("ident_bf", [P, P], BF16)
        ones = sb("ones", [P, P])
        row_mask = sb("row_mask", [P, G, P], BF16)
        col_mask = sb("col_mask", [P, G, P], BF16)
        block_sel3 = sb("block_sel3", [ROWS, 3, G])
        block_sel = sb("block_sel", [ROWS, G])
        pool_gate = sb("pool_gate", [P, 16])
        dve_gate = sb("dve_gate", [P, 1])
        power = sb("power", [P, 4])
        Kraw = sb("Kraw", [P, 3, C])
        KT_hi = sb("KT_hi", [C, 3 * NP], F32R)
        KT_lo = sb("KT_lo", [C, 3 * NP], F32R)
        Vraw = sb("Vraw", [P, 2, C])
        qkV = sb("qkV", [NP, 2, C])
        vV_sb = sb("vV_sb", [NP, C])
        pK_raw = sb("pK_raw", [NP, C])
        pKT = sb("pKT", [C, NP])
        pV_sb = sb("pV_sb", [NP, C])
        fK_raw = sb("fK_raw", [P, KC, C])
        fKT_hi = sb("fKT_hi", [C, NF], F32R)
        fKT_lo = sb("fKT_lo", [C, NF], F32R)
        fV_sb = sb("fV_sb", [P, KC, C])
        W1_raw = sb("W1_raw", [P, FC, C])
        W2_raw = sb("W2_raw", [C, FF])
        W_neg = sb("W_neg", [P, 512])
        W1_q = sb("W1_q", [P, FC, C])
        W2_q = sb("W2_q", [C, FF])
        W1T = sb("W1T", [C, FF], F32R)
        W2T = sb("W2T", [P, FC, C], F32R)
        W_sums = sb("W_sums", [P, 2])
        W_thr = sb("W_thr", [P, 2])
        W_nthr = sb("W_nthr", [P, 2])
        b1_rows = sb("b1_rows", [FC, P])
        b1_sb = sb("b1_sb", [P, FC])
        b2_row = sb("b2_row", [1, C])
        b2_all = sb("b2_all", [P, NT, C])

        x_in = [sb(f"x_in{i}", [P, NT, C]) for i in range(2)]
        x1 = [sb(f"x1_{i}", [P, NT, C]) for i in range(2)]
        q_stats = sb("q_stats", [P, NT, 6])
        q_mv = [sb(f"q_mv{i}", [P, NT, 2]) for i in range(2)]
        q_var = sb("q_var", [P, 2, NT])
        q_rstd = [sb(f"q_rstd{i}", [P, 2, NT]) for i in range(2)]
        h_ln = sb("h_ln", [P, NT, C])
        hT_hi = sb("hT_hi", [C, T], F32R)
        hT_lo = sb("hT_lo", [C, T], F32R)
        q_nmax = sb("q_nmax", [P, NT, 3])
        q_sum = sb("q_sum", [P, NT, 3])
        q_rsum = sb("q_rsum", [P, NT, 3])
        q_exp = sb("q_exp", [P, NT, 3, NP])
        q_prob = sb("q_prob", [P, NT, 2, NP])
        qkT_prob = sb("qkT_prob", [NP, 2, T])
        vT_prob = sb("vT_prob", [NP, T])
        qk_hi = sb("qk_hi", [C, 2, T], F32R)
        qk_lo = sb("qk_lo", [C, 2, T], F32R)
        q_stack = sb("q_stack", [ROWS, G, T], F32R)
        k_stack = [sb(f"k_stack{i}", [P, G, T], F32R) for i in range(2)]
        q_block = [sb(f"q_block{i}", [P, H, T], F32R) for i in range(2)]
        v_head = [sb(f"v_head{i}", [P, NT, H, 32]) for i in range(2)]
        a_nmax = sb("a_nmax", [P, NT, H])
        nmaxT = [sb(f"nmaxT{i}", [H // 2, T], F32R) for i in range(2)]
        probs0 = [sb(f"probs0_{i}", [P, G, T]) for i in range(2)]
        probs1 = [sb(f"probs1_{i}", [P, G, P]) for i in range(2)]
        oT_raw = [sb(f"oT_raw{i}", [P, G, T]) for i in range(2)]
        o_rsum = sb("o_rsum", [P, NT, H])
        o_ln = sb("o_ln", [P, NT, C])
        oT = sb("oT", [C, T])
        p_nmax = sb("p_nmax", [P, NT])
        p_sum = sb("p_sum", [P, NT])
        p_rsum = sb("p_rsum", [P, NT])
        p_exp = sb("p_exp", [P, NT, NP])
        pT_exp = sb("pT_exp", [NP, T])
        y1 = [sb(f"y1_{i}", [P, NT, C]) for i in range(2)]
        p_stats = sb("p_stats", [P, NT, 6])
        p_mv = sb("p_mv", [P, NT, 2])
        p_var = sb("p_var", [P, NT])
        p_rstd = sb("p_rstd", [P, NT])
        f_ln = sb("f_ln", [P, NT, C])
        fT_hi = sb("fT_hi", [C, T], F32R)
        fT_lo = sb("fT_lo", [C, T], F32R)
        m_nmax = sb("m_nmax", [P, NT])
        m_sum = sb("m_sum", [P, NT])
        m_rsum = sb("m_rsum", [P, NT])
        m_exp = sb("m_exp", [P, NT, NF])
        mT_exp = sb("mT_exp", [P, NT, KC, P])
        y2 = sb("y2", [P, NT, C])
        m_stats = sb("m_stats", [P, NT, 6])
        m_mv = sb("m_mv", [P, NT, 2])
        m_var = sb("m_var", [P, NT])
        m_rstd = sb("m_rstd", [P, NT])
        y2_ln = sb("y2_ln", [P, NT, C])
        x_again = sb("x_again", [P, NT, C])
        x2 = [sb(f"x2_{i}", [P, NT, C]) for i in range(2)]
        z_stats = sb("z_stats", [P, NT, 6])
        z_mv = sb("z_mv", [P, NT, 2])
        z_var = sb("z_var", [P, NT])
        z_rstd = sb("z_rstd", [P, NT])
        z_ln = sb("z_ln", [P, NT, C])
        zT_hi = sb("zT_hi", [C, T], F32R)
        zT_lo = sb("zT_lo", [C, T], F32R)
        hidden = sb("hidden", [P, FC, T])
        hidden_hi = sb("hidden_hi", [P, FC, T], F32R)
        hidden_lo = sb("hidden_lo", [P, FC, T], F32R)
        u = sb("u", [P, NT, C])
        u_stats = sb("u_stats", [P, NT, 6])
        u_mv = sb("u_mv", [P, NT, 2])
        u_var = sb("u_var", [P, NT])
        u_rstd = sb("u_rstd", [P, NT])
        u_ln = sb("u_ln", [P, NT, C])
        x_out = [sb(f"x_out{i}", [P, NT, C]) for i in range(2)]

        row_bank = [bank(f"row_bank{i}") for i in range(2)]
        col_bank = [bank(f"col_bank{i}") for i in range(2)]
        pv_bank = bank("pv_bank")
        qkv_bank = bank("qkv_bank")
        mix_bank = bank("mix_bank")
        pf_bank = bank("pf_bank")

        pe_qkv = track("pe_qkv", ["ln_T", "logits0", "logits1", "qk_prob_T", "qk", "v_prob_T", "v"])
        dve_qkv = track("dve_qkv", [
            "stats0", "stats1", "mv0", "mv1", "ln0", "ln1", "lnT_lo", "max0", "max1", "rsum0", "rsum1",
            "qk_lo", "v_prob_T", "v0", "v1", "x1_0", "x1_1"])
        act_qkv = track("act_qkv", ["lnT_hi", "exp0q", "exp0k", "exp0v", "exp1q", "exp1k", "exp1v",
                                    "qk_prob_T", "qk_hi"])
        pool_qkv = track("pool_qkv", ["var", "var2", "rstd", "q0", "k0", "q1", "k1",
                                      "block0", "block1", "block2", "block3"])
        pe_row = track("pe_row", [*[f"row{i}" for i in range(6)], "max_T0",
                                  *[f"row{i}" for i in range(6, 12)], "max_T1"])
        dve_row = track("dve_row", [f"max{i}" for i in range(12)])
        act_row = track("act_row", ["max_T0", "max_T1"])
        pe_col = track("pe_col", [*[f"col{i}" for i in range(5)], "pv0", "col5", "col6", "col7", "pv1",
                                  "col8", "col9", "col10", "pv2", "col11", "pv3"])
        act_col = track("act_col", [*[f"exp{i}" for i in range(8)], "out0", *[f"exp{i}" for i in range(8, 12)],
                                    "out1"])
        pe_proj = track("pe_proj", ["att_T0", "att_T1", "o_T", "logits", "prob_T", "out"])
        dve_proj = track("dve_proj", ["rsum0", "o0", "rsum1", "o1", "max", "prob_T", "rsum", "y0", "y1",
                                      "stats0", "stats1", "mv0", "mv1", "ln0", "ln1"])
        act_proj = track("act_proj", ["o_T", "exp0", "exp1"])
        pool_proj = track("pool_proj", ["var", "rstd"])
        pe_mix = track("pe_mix", ["ln_T", "logits0", "logits1", "prob_T0", "prob_T1", "out"])
        dve_mix = track("dve_mix", ["lnT_lo", "max0", "max1", "rsum", "y0", "y1", "stats0", "stats1",
                                    "mv0", "mv1", "ln0", "ln1", "zstats0", "zstats1", "zmv0", "zmv1",
                                    "z0", "z1"])
        act_mix = track("act_mix", ["lnT_hi", "exp0", "exp1", "prob_T0", "prob_T1"])
        pool_mix = track("pool_mix", ["var", "rstd", "x2", "zvar", "zrstd"])
        pe_ffn = track("pe_ffn", ["z_T", "up0", "up1", "down"])
        dve_ffn = track("dve_ffn", ["zT_lo", "u", "stats0", "stats1", "mv0", "mv1", "ln0", "ln1"])
        act_ffn = track("act_ffn", ["zT_hi", "relu0", "relu1", "relu2", "relu3"])
        pool_ffn = track("pool_ffn", ["hi0", "lo0", "hi1", "lo1", "var", "rstd", "out"])
        x_loaded = [sem(f"x_loaded{i}") for i in range(2)]
        stacked = sem("stacked")
        max_moved = [sem(f"max_moved{i}") for i in range(2)]
        x_reloaded = sem("x_reloaded")
        stored = [sem(f"stored{i}") for i in range(2)]
        first_loads = sem("first_loads")
        late_loads = sem("late_loads")
        consts = sem("consts")
        dve_prep = sem("dve_prep")
        pe_prep = sem("pe_prep")
        act_prep = sem("act_prep")
        STACKS = 6
        CONSTS = 19

        def dram_rows(a, seq):
            flat = a.rearrange("b t c -> (b t) c")
            return flat[bass.ds(seq.number * T, T), :].rearrange("(t p) c -> p t c", p=P)

        def run_steps(eng, step, after_first=None):
            def at(s, number):
                return [Sequence(number - k, (s - k) % 2) if not isinstance(number, int) or 0 <= s - k < B
                        else None for k in range(STAGES)]

            first = STAGES + 1
            for s in range(first):
                step(*at(s, s))
                if s == 0 and after_first:
                    after_first()
            with eng.Fori(first, B - 1, 2) as number:
                step(*at(first, number))
                step(*at(first + 1, number + 1))
            for s in range(B, B + STAGES - 1):
                step(*at(s, s))

        def in_order(pieces):
            for piece, seq, *more in pieces:
                if seq is not None:
                    piece(seq, *more)

        block = ctx.enter_context(nc.Block())

        @block.sync
        def _(sp):
            for i, w in enumerate((qK, kK, vK)):
                sp.dma_start(Kraw[:, i, :], w).then_inc(first_loads, 16)
            for i, w in enumerate((qV, kV)):
                sp.dma_start(Vraw[:, i, :], w).then_inc(first_loads, 16)
            sp.dma_start(vV_sb[:], vV).then_inc(first_loads, 16)

            def load_x(seq):
                if seq.has_before(2):
                    sp.wait_ge(*dve_qkv.at(seq, "x1_1", back=2))
                sp.dma_start(x_in[seq.parity][:], dram_rows(x, seq)).then_inc(x_loaded[seq.parity], 16)

            def stack(seq):
                sp.wait_ge(*dve_qkv.at(seq, "qk_lo"))
                if seq.has_before(1):
                    sp.wait_ge(*pool_qkv.at(seq, "block3", back=1))
                if seq.has_before(2):
                    sp.wait_ge(*pe_col.at(seq, "pv3", back=2))
                for part, (q_part, k_part) in enumerate(((qk_hi, qk_hi), (qk_hi, qk_lo), (qk_lo, qk_hi))):
                    rows = slice(part * G * D, (part + 1) * G * D)
                    sp.dma_start(q_stack[rows].bitcast(F32), q_part[:, 0, :].bitcast(F32)).then_inc(stacked, 16)
                    sp.dma_start(k_stack[seq.parity][rows].bitcast(F32),
                                 k_part[:, 1, :].bitcast(F32)).then_inc(stacked, 16)

            def move_max(seq, half):
                heads = slice(half * H // 2, (half + 1) * H // 2)
                sp.wait_ge(*act_row.at(seq, f"max_T{half}"))
                sp.dma_start(q_block[seq.parity][ROWS:ROWS + 1, heads].bitcast(F32), nmaxT[half][:].bitcast(F32))\
                  .then_inc(max_moved[half], 16)

            def reload_x(seq):
                if seq.has_before(1):
                    sp.wait_ge(*pool_mix.at(seq, "x2", back=1))
                sp.dma_start(x_again[:], dram_rows(x, seq)).then_inc(x_reloaded, 16)

            def store(seq):
                sp.wait_ge(*pool_ffn.at(seq, "out"))
                sp.dma_start(dram_rows(out, seq), x_out[seq.parity][:]).then_inc(stored[seq.parity], 16)

            def step(qkv, attn, proj, mix, ffn):
                in_order([
                    (load_x, qkv), (reload_x, mix), (move_max, attn, 0), (move_max, attn, 1), (stack, qkv),
                    (store, ffn)])

            run_steps(sp, step)
            for i in range(2):
                sp.wait_ge(stored[i], 16 * B // 2)

        @block.gpsimd
        def _(pool):
            for dst, src in ((pK_raw[:], pK), (pV_sb[:], pV),
                             (fK_raw[:], fK.rearrange("(a p) c -> p a c", p=P)),
                             (fV_sb[:], fV.rearrange("(a p) c -> p a c", p=P)),
                             (W1_raw[:], W1.rearrange("(a p) c -> p a c", p=P)),
                             (W2_raw[:], W2),
                             (b1_rows[:], b1.rearrange("(a p) -> a p", p=P)),
                             (b2_row[:], b2.rearrange("(a c) -> a c", a=1))):
                nc.gpsimd.dma_start(dst, src).then_inc(late_loads, 16)
            nc.gpsimd.memset(ident[:], 0.0).then_inc(consts, 1)
            nc.gpsimd.memset(ident_bf[:], 0.0).then_inc(consts, 1)
            nc.gpsimd.memset(power[:], -0.5).then_inc(consts, 1)
            nc.gpsimd.memset(row_mask[:], 0.0).then_inc(consts, 1)
            nc.gpsimd.memset(col_mask[:], 0.0).then_inc(consts, 1)
            nc.gpsimd.memset(block_sel3[:], 1.0).then_inc(consts, 1)
            nc.gpsimd.memset(ones[:], 1.0).then_inc(consts, 1)
            pool.wait_ge(consts, 7)
            nc.gpsimd.affine_select(out=ident[:], in_=ident[:], compare_op=ALU.not_equal, fill=1.0, base=0,
                                    pattern=[[-1, P]], channel_multiplier=1).then_inc(consts, 1)
            nc.gpsimd.affine_select(out=ident_bf[:], in_=ident_bf[:], compare_op=ALU.not_equal, fill=1.0,
                                    base=0, pattern=[[-1, P]], channel_multiplier=1).then_inc(consts, 1)
            nc.gpsimd.affine_select(out=row_mask[:], in_=row_mask[:], compare_op=ALU.is_ge, fill=MASKED,
                                    base=0, pattern=[[0, G], [-1, P]], channel_multiplier=1).then_inc(consts, 1)
            nc.gpsimd.affine_select(out=col_mask[:], in_=col_mask[:], compare_op=ALU.is_ge, fill=MASKED,
                                    base=0, pattern=[[0, G], [1, P]], channel_multiplier=-1).then_inc(consts, 1)
            nc.gpsimd.affine_select(out=block_sel3[:], in_=block_sel3[:], compare_op=ALU.is_ge, fill=0.0,
                                    base=0, pattern=[[-G * D, 3], [-D, G]], channel_multiplier=1)\
                .then_inc(consts, 1)
            pool.wait_ge(consts, 12)
            nc.gpsimd.affine_select(out=block_sel3[:], in_=block_sel3[:], compare_op=ALU.is_ge, fill=0.0,
                                    base=D - 1, pattern=[[G * D, 3], [D, G]], channel_multiplier=-1)\
                .then_inc(consts, 1)
            for i in range(2):
                nc.gpsimd.memset(v_head[i][:], 0.0).then_inc(consts, 1)
            pool.wait_ge(consts, 15)
            for i in range(2):
                nc.gpsimd.memset(k_stack[i][ROWS:ROWS + 1, :, :].bitcast(F32), 1.0).then_inc(consts, 1)
            pool.wait_ge(consts, 17)
            for i in range(2):
                nc.gpsimd.memset(v_head[i][:, :, :, D:D + 1], 1.0).then_inc(consts, 1)

            gates = iter(range(1000))

            def gate():
                n = next(gates) % pool_gate.shape[1]
                nc.gpsimd.tensor_tensor(pool_gate[:, n:n + 1], power[:, 0:1], power[:, 0:1], ALU.mult)

            def qkv_rstd(seq):
                pool.wait_ge(*dve_qkv.at(seq, "mv1"))
                gate()
                mv = q_mv[seq.parity]
                nc.gpsimd.tensor_scalar(q_var[:, 0, :], mv[:, :, 1], 1.0, EPS, ALU.mult, ALU.add)\
                    .then_inc(*pool_qkv.done("var"))
                nc.gpsimd.tensor_scalar(q_var[:, 1, :], mv[:, :, 1], 1.0 + EPS, EPS * EPS, ALU.mult, ALU.add)\
                    .then_inc(*pool_qkv.done("var2"))
                pool.wait_ge(*pool_qkv.at(seq, "var2"))
                if seq.has_before(2):
                    pool.wait_ge(*dve_qkv.at(seq, "x1_1", back=2))
                nc.gpsimd.tensor_tensor(q_rstd[seq.parity][:].rearrange("p a b -> p (a b)"),
                                        q_var[:].rearrange("p a b -> p (a b)"), power[:, 0:4], ALU.pow)\
                    .then_inc(*pool_qkv.done("rstd"))

            def qk_probs(seq, t):
                pool.wait_ge(*dve_qkv.at(seq, f"rsum{t}"))
                if seq.has_before(1):
                    pool.wait_ge(*pe_qkv.at(seq, "qk_prob_T", back=1))
                gate()
                for i, which in enumerate("qk"):
                    nc.gpsimd.tensor_scalar(q_prob[:, t, i, :], q_exp[:, t, i, :], q_rsum[:, t, i:i + 1], 1.0,
                                            ALU.mult, ALU.mult).then_inc(*pool_qkv.done(f"{which}{t}"))

            def q_blocks(seq, j):
                if j == 0:
                    pool.wait_ge(stacked, seq.dmas(STACKS))
                    if seq.has_before(2):
                        pool.wait_ge(*pe_col.at(seq, "pv3", back=2))
                    gate()
                nc.gpsimd.tensor_scalar(q_block[seq.parity][0:ROWS, G * j:G * j + G, :],
                                        q_stack[:].bitcast(F32), block_sel[:, j:j + 1], 1.0,
                                        ALU.mult, ALU.mult).then_inc(*pool_qkv.done(f"block{j}"))

            def rstd(seq, stage, var_of, names, mv, var, out_, readers):
                pool.wait_ge(*var_of)
                if readers:
                    pool.wait_ge(*readers)
                gate()
                nc.gpsimd.tensor_scalar(var[:], mv[:, :, 1], 1.0, EPS, ALU.mult, ALU.add)\
                    .then_inc(*stage.done(names[0]))
                pool.wait_ge(*stage.at(seq, names[0]))
                nc.gpsimd.tensor_tensor(out_[:], var[:], power[:, 0:NT], ALU.pow).then_inc(*stage.done(names[1]))

            def proj_rstd(seq):
                rstd(seq, pool_proj, dve_proj.at(seq, "mv1"), ("var", "rstd"), p_mv, p_var, p_rstd, None)

            def mix_rstd(seq):
                rstd(seq, pool_mix, dve_mix.at(seq, "mv1"), ("var", "rstd"), m_mv, m_var, m_rstd, None)

            def add_x2(seq):
                pool.wait_ge(*dve_mix.at(seq, "ln1"))
                pool.wait_ge(x_reloaded, seq.dmas(1))
                if seq.has_before(2):
                    pool.wait_ge(*pool_ffn.at(seq, "out", back=2))
                nc.gpsimd.tensor_tensor(x2[seq.parity][:], y2_ln[:], x_again[:], ALU.add)\
                    .then_inc(*pool_mix.done("x2"))

            def z_rstd_(seq):
                rstd(seq, pool_mix, dve_mix.at(seq, "zmv1"), ("zvar", "zrstd"), z_mv, z_var, z_rstd, None)

            def split_hidden(seq, half):
                pool.wait_ge(*act_ffn.at(seq, f"relu{2 * half + 1}"))
                if seq.has_before(1):
                    pool.wait_ge(*pe_ffn.at(seq, "down", back=1))
                gate()
                part = slice(2 * half, 2 * half + 2)
                nc.gpsimd.tensor_copy(hidden_hi[:, part, :], hidden[:, part, :]).then_inc(*pool_ffn.done(f"hi{half}"))
                pool.wait_ge(*pool_ffn.at(seq, f"hi{half}"))
                nc.gpsimd.tensor_tensor(hidden_lo[:, part, :], hidden[:, part, :], hidden_hi[:, part, :].bitcast(F32),
                                        ALU.subtract).then_inc(*pool_ffn.done(f"lo{half}"))

            def ffn_rstd(seq):
                rstd(seq, pool_ffn, dve_ffn.at(seq, "mv1"), ("var", "rstd"), u_mv, u_var, u_rstd, None)

            def add_out(seq):
                pool.wait_ge(*dve_ffn.at(seq, "ln1"))
                if seq.has_before(2):
                    pool.wait_ge(stored[seq.parity], seq.dmas_of_parity(back=2))
                nc.gpsimd.tensor_tensor(x_out[seq.parity][:], u_ln[:], x2[seq.parity][:], ALU.add)\
                    .then_inc(*pool_ffn.done("out"))

            def step(qkv, attn, proj, mix, ffn):
                in_order([
                    (qkv_rstd, qkv), (split_hidden, ffn, 0), (qk_probs, qkv, 0), (qk_probs, qkv, 1),
                    (split_hidden, ffn, 1), (mix_rstd, mix), (add_x2, mix), (z_rstd_, mix), (ffn_rstd, ffn),
                    (proj_rstd, proj), (add_out, ffn), (q_blocks, qkv, 0), (q_blocks, qkv, 1), (q_blocks, qkv, 2),
                    (q_blocks, qkv, 3)])

            run_steps(pool, step)

        @block.scalar
        def _(act):
            def copy(dst, src, scale=1.0):
                return nc.scalar.activation(dst, src, ACT.Copy, scale=scale)

            act.wait_ge(pe_prep, 1)
            copy(KT_hi[:], qkv_bank[:, 0:3 * NP], scale=SCALE).then_inc(act_prep, 1)

            def prep_rest():
                act.wait_ge(pe_prep, 2)
                copy(fKT_hi[:], mix_bank[:], scale=SCALE).then_inc(act_prep, 1)
                act.wait_ge(pe_prep, 3)
                copy(pKT[:], pf_bank[:, 0:NP], scale=SCALE).then_inc(act_prep, 1)
                act.wait_ge(dve_prep, 7)
                act.wait_ge(pe_prep, 5)
                copy(W1T[:], mix_bank[:]).then_inc(act_prep, 1)
                act.wait_ge(pe_prep, 6)
                copy(W2T[:].rearrange("p a c -> p (a c)"), pv_bank[:]).then_inc(act_prep, 1)

            def qkv_lnT(seq):
                act.wait_ge(*pe_qkv.at(seq, "ln_T"))
                copy(hT_hi[:], qkv_bank[:, 0:T]).then_inc(*act_qkv.done("lnT_hi"))

            def qkv_exp(seq, t):
                act.wait_ge(*dve_qkv.at(seq, f"max{t}"))
                if seq.has_before(1):
                    act.wait_ge(*pool_qkv.at(seq, f"k{t}", back=1))
                    act.wait_ge(*pe_qkv.at(seq, "v_prob_T", back=1))
                for i, which in enumerate("qkv"):
                    nc.scalar.activation(q_exp[:, t, i, :], qkv_bank[:, i * NP:(i + 1) * NP], ACT.Exp,
                                         bias=q_nmax[:, t, i:i + 1], accum_out=q_sum[:, t, i:i + 1])\
                      .then_inc(*act_qkv.done(f"exp{t}{which}"))

            def qk_prob_T(seq):
                act.wait_ge(*pe_qkv.at(seq, "qk_prob_T"))
                copy(qkT_prob[:].rearrange("p a b -> p (a b)"), qkv_bank[:]).then_inc(*act_qkv.done("qk_prob_T"))

            def qk_high(seq):
                act.wait_ge(*pe_qkv.at(seq, "qk"))
                if seq.has_before(1):
                    act.wait_ge(stacked, seq.dmas(STACKS, back=1))
                copy(qk_hi[:].rearrange("p a b -> p (a b)"), qkv_bank[:]).then_inc(*act_qkv.done("qk_hi"))

            def max_T(seq, half):
                act.wait_ge(*pe_row.at(seq, f"max_T{half}"))
                if seq.has_before(1):
                    act.wait_ge(max_moved[half], seq.dmas(1, back=1))
                copy(nmaxT[half][:], row_bank[half][0:H // 2, 0:T]).then_inc(*act_row.done(f"max_T{half}"))

            def attn_exp(seq, i):
                act.wait_ge(*pe_col.at(seq, f"col{i}"))
                j, kind = divmod(i, 3)
                src = col_bank[i % 2]
                if kind < 2:
                    dst = probs0[j % 2][:, 2 * kind:2 * kind + 2, :].rearrange("p a b -> p (a b)")
                else:
                    dst = probs1[j % 2][:].rearrange("p a b -> p (a b)")
                nc.scalar.activation(dst, src[:], ACT.Exp).then_inc(*act_col.done(f"exp{i}"))

            def attn_out(seq, half):
                act.wait_ge(*pe_col.at(seq, f"pv{2 * half + 1}"))
                if seq.has_before(2):
                    act.wait_ge(*pe_proj.at(seq, "att_T1", back=2))
                copy(oT_raw[seq.parity][:, 2 * half:2 * half + 2, :].rearrange("p a b -> p (a b)"), pv_bank[:])\
                    .then_inc(*act_col.done(f"out{half}"))

            def proj_o_T(seq):
                act.wait_ge(*pe_proj.at(seq, "o_T"))
                copy(oT[:], pf_bank[:, 0:T]).then_inc(*act_proj.done("o_T"))

            def proj_exp(seq):
                act.wait_ge(*dve_proj.at(seq, "max"))
                if seq.has_before(1):
                    act.wait_ge(*pe_proj.at(seq, "prob_T", back=1))
                for t in range(NT):
                    nc.scalar.activation(p_exp[:, t, :], pf_bank[:, t * NP:(t + 1) * NP], ACT.Exp,
                                         bias=p_nmax[:, t:t + 1], accum_out=p_sum[:, t:t + 1])\
                      .then_inc(*act_proj.done(f"exp{t}"))

            def mix_lnT(seq):
                act.wait_ge(*pe_mix.at(seq, "ln_T"))
                copy(fT_hi[:], mix_bank[:, 0:T]).then_inc(*act_mix.done("lnT_hi"))

            def mix_exp(seq, t):
                act.wait_ge(*dve_mix.at(seq, f"max{t}"))
                if seq.has_before(1):
                    act.wait_ge(*pe_mix.at(seq, f"prob_T{t}", back=1))
                nc.scalar.activation(m_exp[:, t, :], mix_bank[:], ACT.Exp, bias=m_nmax[:, t:t + 1],
                                     accum_out=m_sum[:, t:t + 1]).then_inc(*act_mix.done(f"exp{t}"))

            def mix_prob_T(seq, t):
                act.wait_ge(*pe_mix.at(seq, f"prob_T{t}"))
                copy(mT_exp[:, t].rearrange("p a b -> p (a b)"), mix_bank[:]).then_inc(*act_mix.done(f"prob_T{t}"))

            def ffn_zT(seq):
                act.wait_ge(*pe_ffn.at(seq, "z_T"))
                copy(zT_hi[:], pf_bank[:, 0:T]).then_inc(*act_ffn.done("zT_hi"))

            def ffn_relu(seq, half):
                act.wait_ge(*pe_ffn.at(seq, f"up{half}"))
                if seq.has_before(1):
                    act.wait_ge(*pool_ffn.at(seq, f"lo{half}", back=1))
                for i in range(2):
                    a = 2 * half + i
                    nc.scalar.activation(hidden[:, a, :], pf_bank[:, i * T:(i + 1) * T], ACT.Relu,
                                         bias=b1_sb[:, a:a + 1]).then_inc(*act_ffn.done(f"relu{a}"))

            def step(qkv, attn, proj, mix, ffn):
                in_order([
                    (mix_lnT, mix), (mix_exp, mix, 0), (ffn_zT, ffn), (qkv_lnT, qkv), (proj_o_T, proj),
                    (mix_exp, mix, 1), (ffn_relu, ffn, 0), (mix_prob_T, mix, 0), (max_T, attn, 0), (qkv_exp, qkv, 0),
                    (proj_exp, proj), (mix_prob_T, mix, 1), (qkv_exp, qkv, 1), (ffn_relu, ffn, 1),
                    (attn_exp, attn, 0), (attn_exp, attn, 1), (attn_exp, attn, 2), (qk_prob_T, qkv), (qk_high, qkv),
                    (max_T, attn, 1), (attn_exp, attn, 3), (attn_exp, attn, 4), (attn_exp, attn, 5),
                    (attn_exp, attn, 6), (attn_exp, attn, 7), (attn_exp, attn, 8), (attn_out, attn, 0),
                    (attn_exp, attn, 9), (attn_exp, attn, 10), (attn_exp, attn, 11), (attn_out, attn, 1)])

            run_steps(act, step, prep_rest)

        @block.vector
        def _(dve):
            def flat(ap):
                return ap.rearrange("p a b -> p (a b)")

            dve.wait_ge(first_loads, 16 * 6)
            for i, scale in enumerate((float(D) ** -0.5, 1.0)):
                nc.vector.tensor_scalar(qkV[:, i, :].rearrange("p (j d g) -> p j d g", j=G, d=D, g=G),
                                        Vraw[:, i, :].rearrange("p (j g d) -> p j d g", j=G, d=D, g=G),
                                        scale, None, ALU.mult).then_inc(dve_prep, 1)
            dve.wait_ge(consts, CONSTS)
            nc.vector.tensor_reduce(block_sel[:], block_sel3[:].rearrange("p a b -> p b a"), axis=AX.X,
                                    op=ALU.add).then_inc(dve_prep, 1)
            dve.wait_ge(act_prep, 1)
            nc.vector.scalar_tensor_tensor(KT_lo[:], qkv_bank[:, 0:3 * NP], SCALE, KT_hi[:].bitcast(F32),
                                           ALU.mult, ALU.subtract).then_inc(dve_prep, 1)

            def prep_rest():
                dve.wait_ge(late_loads, 16 * 8)
                nc.vector.tensor_reduce(W_sums[:, 0:1], flat(W1_raw[:]), axis=AX.X, op=ALU.add,
                                        apply_absolute_value=True).then_inc(dve_prep, 1)
                nc.vector.tensor_reduce(W_sums[:, 1:2], W2_raw[:], axis=AX.X, op=ALU.add,
                                        apply_absolute_value=True).then_inc(dve_prep, 1)
                dve.wait_ge(act_prep, 2)
                nc.vector.scalar_tensor_tensor(fKT_lo[:], mix_bank[:], SCALE, fKT_hi[:].bitcast(F32),
                                               ALU.mult, ALU.subtract).then_inc(dve_prep, 1)
                dve.wait_ge(act_prep, 3)
                dve.wait_ge(pe_prep, 4)
                nc.vector.tensor_scalar(W_thr[:], pf_bank[:, 0:2], 0.5 / (FF * C), 0.5 * EPS, ALU.mult, ALU.add)\
                  .then_inc(dve_prep, 1)
                dve.wait_ge(dve_prep, 8)
                nc.vector.tensor_scalar(W_nthr[:], W_thr[:], -1.0, None, ALU.mult).then_inc(dve_prep, 1)
                nc.vector.tensor_copy(b1_sb[:], pf_bank[:, 2 * P:2 * P + FC]).then_inc(dve_prep, 1)
                for t in range(NT):
                    nc.vector.tensor_copy(b2_all[:, t, :], pf_bank[:, P:2 * P]).then_inc(dve_prep, 1)
                dve.wait_ge(dve_prep, 9)
                nc.vector.tensor_scalar(W_neg[:], flat(W1_raw[:]), W_nthr[:, 0:1], None, ALU.is_lt)\
                  .then_inc(dve_prep, 1)
                dve.wait_ge(dve_prep, 13)
                nc.vector.scalar_tensor_tensor(flat(W1_q[:]), flat(W1_raw[:]), W_thr[:, 0:1], W_neg[:],
                                               ALU.is_gt, ALU.subtract).then_inc(dve_prep, 1)
                dve.wait_ge(dve_prep, 14)
                nc.vector.tensor_scalar(W_neg[:], W2_raw[:], W_nthr[:, 1:2], None, ALU.is_lt)\
                  .then_inc(dve_prep, 1)
                dve.wait_ge(dve_prep, 15)
                nc.vector.scalar_tensor_tensor(W2_q[:], W2_raw[:], W_thr[:, 1:2], W_neg[:],
                                               ALU.is_gt, ALU.subtract).then_inc(dve_prep, 1)

            def norm_stats(seq, src, stats, mv, stage, prefix=""):
                for t in range(NT):
                    nc.vector.bn_stats(stats[:, t, :], src[:, t, :]).then_inc(*stage.done(f"{prefix}stats{t}"))
                dve.wait_ge(*stage.at(seq, f"{prefix}stats{NT - 1}"))
                nc.vector.memset(dve_gate[:], 0.0)
                for t in range(NT):
                    nc.vector.bn_aggr(mv[:, t, :], stats[:, t, :]).then_inc(*stage.done(f"{prefix}mv{t}"))

            def normalise(dst, src, mv, rstd, t):
                return nc.vector.tensor_scalar(dst, src, mv[:, t, 0:1], rstd[:, t:t + 1], ALU.subtract, ALU.mult)

            def qkv_stats(seq):
                dve.wait_ge(x_loaded[seq.parity], seq.dmas_of_parity())
                norm_stats(seq, x_in[seq.parity], q_stats, q_mv[seq.parity], dve_qkv)

            def qkv_ln(seq):
                dve.wait_ge(*pool_qkv.at(seq, "rstd"))
                if seq.has_before(1):
                    dve.wait_ge(*pe_qkv.at(seq, "ln_T", back=1))
                for t in range(NT):
                    normalise(h_ln[:, t, :], x_in[seq.parity][:, t, :], q_mv[seq.parity],
                              q_rstd[seq.parity][:, 1, :], t).then_inc(*dve_qkv.done(f"ln{t}"))

            def qkv_lnT(seq):
                dve.wait_ge(*act_qkv.at(seq, "lnT_hi"))
                if seq.has_before(1):
                    dve.wait_ge(*pe_qkv.at(seq, "logits1", back=1))
                nc.vector.tensor_tensor(hT_lo[:], qkv_bank[:, 0:T], hT_hi[:].bitcast(F32), ALU.subtract)\
                  .then_inc(*dve_qkv.done("lnT_lo"))

            def qkv_max(seq, t):
                dve.wait_ge(*pe_qkv.at(seq, f"logits{t}"))
                nc.vector.tensor_reduce(q_nmax[:, t, :], qkv_bank[:, 0:3 * NP].rearrange("p (a b) -> p a b", a=3),
                                        axis=AX.X, op=ALU.max, negate=True).then_inc(*dve_qkv.done(f"max{t}"))

            def qkv_rsum(seq, t):
                dve.wait_ge(*act_qkv.at(seq, f"exp{t}v"))
                nc.vector.reciprocal(q_rsum[:, t, :], q_sum[:, t, :]).then_inc(*dve_qkv.done(f"rsum{t}"))

            def qk_low(seq):
                dve.wait_ge(*act_qkv.at(seq, "qk_hi"))
                nc.vector.tensor_tensor(flat(qk_lo[:]), qkv_bank[:], flat(qk_hi[:]).bitcast(F32), ALU.subtract)\
                  .then_inc(*dve_qkv.done("qk_lo"))

            def v_prob_T(seq):
                dve.wait_ge(*pe_qkv.at(seq, "v_prob_T"))
                nc.vector.tensor_copy(vT_prob[:], qkv_bank[:, 0:T]).then_inc(*dve_qkv.done("v_prob_T"))

            def v_out(seq):
                dve.wait_ge(*pe_qkv.at(seq, "v"))
                if seq.has_before(2):
                    dve.wait_ge(*pe_col.at(seq, "pv3", back=2))
                for t in range(NT):
                    nc.vector.tensor_scalar(v_head[seq.parity][:, t, :, 0:D],
                                            qkv_bank[:, t * P:(t + 1) * P].rearrange("p (h d) -> p h d", d=D),
                                            q_rsum[:, t, 2:3], None, ALU.mult).then_inc(*dve_qkv.done(f"v{t}"))

            def keep_x1(seq):
                for t in range(NT):
                    normalise(x1[seq.parity][:, t, :], x_in[seq.parity][:, t, :], q_mv[seq.parity],
                              q_rstd[seq.parity][:, 0, :], t).then_inc(*dve_qkv.done(f"x1_{t}"))

            def attn_max(seq, i):
                dve.wait_ge(*pe_row.at(seq, f"row{i}"))
                j, kind = divmod(i, 3)
                src = row_bank[(i + i // 6) % 2]
                if kind < 2:
                    h = G * j + 2 * kind
                    nc.vector.tensor_reduce(a_nmax[:, 1, h:h + 2], src[:].rearrange("p (a b) -> p a b", a=2),
                                            axis=AX.X, op=ALU.max, negate=True).then_inc(*dve_row.done(f"max{i}"))
                else:
                    nc.vector.tensor_reduce(a_nmax[:, 0, G * j:G * j + G], src[:].rearrange("p (a b) -> p a b", a=G),
                                            axis=AX.X, op=ALU.max, negate=True).then_inc(*dve_row.done(f"max{i}"))

            def proj_o(seq, t):
                dve.wait_ge(*pe_proj.at(seq, f"att_T{t}"))
                heads = pf_bank[:].rearrange("p (h r) -> p h r", r=32)
                nc.vector.reciprocal(o_rsum[:, t, :], heads[:, :, D]).then_inc(*dve_proj.done(f"rsum{t}"))
                dve.wait_ge(*dve_proj.at(seq, f"rsum{t}"))
                nc.vector.tensor_tensor(o_ln[:, t, :].rearrange("p (h d) -> p h d", d=D), heads[:, :, 0:D],
                                        o_rsum[:, t, :].unsqueeze(2).broadcast_to([P, H, D]), ALU.mult)\
                  .then_inc(*dve_proj.done(f"o{t}"))

            def proj_max(seq):
                dve.wait_ge(*pe_proj.at(seq, "logits"))
                nc.vector.tensor_reduce(p_nmax[:], pf_bank[:, 0:T].rearrange("p (a b) -> p a b", a=NT),
                                        axis=AX.X, op=ALU.max, negate=True).then_inc(*dve_proj.done("max"))

            def proj_prob_T(seq):
                dve.wait_ge(*pe_proj.at(seq, "prob_T"))
                nc.vector.tensor_copy(pT_exp[:], pf_bank[:, 0:T]).then_inc(*dve_proj.done("prob_T"))

            def residual(seq, stage, src, rsum, sums, add, dst):
                nc.vector.reciprocal(rsum[:], sums[:]).then_inc(*stage.done("rsum"))
                dve.wait_ge(*stage.at(seq, "rsum"))
                for t in range(NT):
                    nc.vector.scalar_tensor_tensor(dst[:, t, :], src[:, t * P:(t + 1) * P], rsum[:, t:t + 1],
                                                   add[:, t, :], ALU.mult, ALU.add).then_inc(*stage.done(f"y{t}"))

            def proj_y1(seq):
                dve.wait_ge(*pe_proj.at(seq, "out"))
                dve.wait_ge(*dve_qkv.at(seq, "x1_1"))
                residual(seq, dve_proj, pf_bank, p_rsum, p_sum, x1[seq.parity], y1[seq.parity])

            def proj_stats(seq):
                dve.wait_ge(*dve_proj.at(seq, "y1"))
                norm_stats(seq, y1[seq.parity], p_stats, p_mv, dve_proj)

            def proj_ln(seq):
                dve.wait_ge(*pool_proj.at(seq, "rstd"))
                if seq.has_before(1):
                    dve.wait_ge(*pe_mix.at(seq, "ln_T", back=1))
                for t in range(NT):
                    normalise(f_ln[:, t, :], y1[seq.parity][:, t, :], p_mv, p_rstd, t)\
                        .then_inc(*dve_proj.done(f"ln{t}"))

            def mix_lnT(seq):
                dve.wait_ge(*act_mix.at(seq, "lnT_hi"))
                nc.vector.tensor_tensor(fT_lo[:], mix_bank[:, 0:T], fT_hi[:].bitcast(F32), ALU.subtract)\
                  .then_inc(*dve_mix.done("lnT_lo"))

            def mix_max(seq, t):
                dve.wait_ge(*pe_mix.at(seq, f"logits{t}"))
                nc.vector.tensor_reduce(m_nmax[:, t:t + 1], mix_bank[:], axis=AX.X, op=ALU.max, negate=True)\
                  .then_inc(*dve_mix.done(f"max{t}"))

            def mix_y2(seq):
                dve.wait_ge(*pe_mix.at(seq, "out"))
                residual(seq, dve_mix, mix_bank, m_rsum, m_sum, y1[seq.parity], y2)

            def mix_stats(seq):
                dve.wait_ge(*dve_mix.at(seq, "y1"))
                norm_stats(seq, y2, m_stats, m_mv, dve_mix)

            def mix_ln(seq):
                dve.wait_ge(*pool_mix.at(seq, "rstd"))
                if seq.has_before(1):
                    dve.wait_ge(*pool_mix.at(seq, "x2", back=1))
                for t in range(NT):
                    normalise(y2_ln[:, t, :], y2[:, t, :], m_mv, m_rstd, t).then_inc(*dve_mix.done(f"ln{t}"))

            def z_stats_(seq):
                dve.wait_ge(*pool_mix.at(seq, "x2"))
                norm_stats(seq, x2[seq.parity], z_stats, z_mv, dve_mix, "z")

            def z_norm(seq):
                dve.wait_ge(*pool_mix.at(seq, "zrstd"))
                if seq.has_before(1):
                    dve.wait_ge(*pe_ffn.at(seq, "z_T", back=1))
                for t in range(NT):
                    normalise(z_ln[:, t, :], x2[seq.parity][:, t, :], z_mv, z_rstd, t)\
                        .then_inc(*dve_mix.done(f"z{t}"))

            def ffn_zT(seq):
                dve.wait_ge(*act_ffn.at(seq, "zT_hi"))
                nc.vector.tensor_tensor(zT_lo[:], pf_bank[:, 0:T], zT_hi[:].bitcast(F32), ALU.subtract)\
                  .then_inc(*dve_ffn.done("zT_lo"))

            def ffn_u(seq):
                dve.wait_ge(*pe_ffn.at(seq, "down"))
                nc.vector.tensor_tensor(flat(u[:]), pf_bank[:, 0:NT * C], flat(b2_all[:]), ALU.add)\
                  .then_inc(*dve_ffn.done("u"))

            def ffn_stats(seq):
                dve.wait_ge(*dve_ffn.at(seq, "u"))
                norm_stats(seq, u, u_stats, u_mv, dve_ffn)

            def ffn_ln(seq):
                dve.wait_ge(*pool_ffn.at(seq, "rstd"))
                if seq.has_before(1):
                    dve.wait_ge(*pool_ffn.at(seq, "out", back=1))
                for t in range(NT):
                    normalise(u_ln[:, t, :], u[:, t, :], u_mv, u_rstd, t).then_inc(*dve_ffn.done(f"ln{t}"))

            def step(qkv, attn, proj, mix, ffn):
                in_order([
                    (qkv_stats, qkv), (attn_max, attn, 0), (mix_lnT, mix), (proj_o, proj, 0), (attn_max, attn, 1),
                    (mix_max, mix, 0), (proj_o, proj, 1), (qkv_ln, qkv), (attn_max, attn, 2), (ffn_zT, ffn),
                    (attn_max, attn, 3), (mix_max, mix, 1), (qkv_lnT, qkv), (attn_max, attn, 4), (attn_max, attn, 5),
                    (qkv_max, qkv, 0), (attn_max, attn, 6), (proj_max, proj), (attn_max, attn, 7), (qkv_max, qkv, 1),
                    (qkv_rsum, qkv, 0), (qkv_rsum, qkv, 1), (attn_max, attn, 8), (attn_max, attn, 9), (mix_y2, mix),
                    (mix_stats, mix), (proj_prob_T, proj), (attn_max, attn, 10), (attn_max, attn, 11), (mix_ln, mix),
                    (ffn_u, ffn), (qk_low, qkv), (z_stats_, mix), (ffn_stats, ffn), (proj_y1, proj), (v_prob_T, qkv),
                    (proj_stats, proj), (z_norm, mix), (ffn_ln, ffn), (v_out, qkv), (proj_ln, proj), (keep_x1, qkv)])

            run_steps(dve, step, prep_rest)

        @block.tensor
        def _(pe):
            mm = nc.tensor.matmul

            pe.wait_ge(consts, CONSTS)
            pe.wait_ge(first_loads, 16 * 6)
            for i in range(3):
                last = nc.tensor.transpose(qkv_bank[:, i * NP:(i + 1) * NP], Kraw[:, i, :], ident[:])
            last.then_inc(pe_prep, 1)

            def prep_rest():
                pe.wait_ge(late_loads, 16 * 8)
                for a in range(KC):
                    last = nc.tensor.transpose(mix_bank[:, a * P:(a + 1) * P], fK_raw[:, a, :], ident[:])
                last.then_inc(pe_prep, 1)
                nc.tensor.transpose(pf_bank[:, 0:NP], pK_raw[:], ident[:]).then_inc(pe_prep, 1)
                pe.wait_ge(act_prep, 3)
                pe.wait_ge(dve_prep, 6)
                mm(pf_bank[:, 0:2], ones[:], W_sums[:], start=True, stop=True)
                mm(pf_bank[:, P:2 * P], ones[0:1, :], b2_row[:], start=True, stop=True)
                nc.tensor.transpose(pf_bank[:, 2 * P:2 * P + FC], b1_rows[:], ident[0:FC, 0:FC])\
                    .then_inc(pe_prep, 1)
                pe.wait_ge(dve_prep, 16)
                for a in range(FC):
                    last = nc.tensor.transpose(mix_bank[:, a * P:(a + 1) * P], W1_q[:, a, :], ident[:])
                last.then_inc(pe_prep, 1)
                for a in range(FC):
                    last = nc.tensor.transpose(pv_bank[:, a * P:(a + 1) * P], W2_q[:, a * P:(a + 1) * P], ident[:])
                last.then_inc(pe_prep, 1)

            def transposes(bank_, srcs):
                for i, src in enumerate(srcs):
                    last = nc.tensor.transpose(bank_[:, i * P:(i + 1) * P], src, ident[:])
                return last

            def three_products(out_, hi, lo, w_hi, w_lo):
                mm(out_, hi, w_hi, start=True, stop=False)
                mm(out_, hi, w_lo, start=False, stop=False)
                return mm(out_, lo, w_hi, start=False, stop=True)

            def qkv_ln_T(seq):
                pe.wait_ge(*dve_qkv.at(seq, "ln1"))
                if seq.has_before(1):
                    pe.wait_ge(*dve_qkv.at(seq, "v1", back=1))
                else:
                    pe.wait_ge(dve_prep, 4)
                transposes(qkv_bank, [h_ln[:, t, :] for t in range(NT)]).then_inc(*pe_qkv.done("ln_T"))

            def qkv_logits(seq, t):
                if t == 0:
                    pe.wait_ge(*dve_qkv.at(seq, "lnT_lo"))
                else:
                    pe.wait_ge(*act_qkv.at(seq, f"exp{t - 1}v"))
                tok = slice(t * P, (t + 1) * P)
                three_products(qkv_bank[:, 0:3 * NP], hT_hi[:, tok], hT_lo[:, tok], KT_hi[:], KT_lo[:])\
                    .then_inc(*pe_qkv.done(f"logits{t}"))

            def qk_prob_T(seq):
                pe.wait_ge(*act_qkv.at(seq, "exp1v"))
                pe.wait_ge(*pool_qkv.at(seq, "k1"))
                transposes(qkv_bank, [q_prob[:, t, i, :] for i in range(2) for t in range(NT)])\
                    .then_inc(*pe_qkv.done("qk_prob_T"))

            def qk(seq):
                pe.wait_ge(*act_qkv.at(seq, "qk_prob_T"))
                for i in range(2):
                    last = mm(qkv_bank[:, i * T:(i + 1) * T], qkV[:, i, :], qkT_prob[:, i, :], start=True, stop=True)
                last.then_inc(*pe_qkv.done("qk"))

            def v_prob_T(seq):
                pe.wait_ge(*dve_qkv.at(seq, "qk_lo"))
                transposes(qkv_bank, [q_exp[:, t, 2, :] for t in range(NT)]).then_inc(*pe_qkv.done("v_prob_T"))

            def v(seq):
                pe.wait_ge(*dve_qkv.at(seq, "v_prob_T"))
                for t in range(NT):
                    last = mm(qkv_bank[:, t * C:(t + 1) * C], vT_prob[:, t * P:(t + 1) * P], vV_sb[:],
                              start=True, stop=True)
                last.then_inc(*pe_qkv.done("v"))

            def row_bank_free(seq, use):
                readers = [*[(dve_row, f"max{i}") for i in range(6)], (act_row, "max_T0"),
                           *[(dve_row, f"max{i}") for i in range(6, 12)], (act_row, "max_T1")]
                reader, name = readers[use - 2]
                if use >= 2:
                    pe.wait_ge(*reader.at(seq, name))
                elif seq.has_before(1):
                    pe.wait_ge(*reader.at(seq, name, back=1))

            def row(seq, i):
                if i == 0:
                    pe.wait_ge(stacked, seq.dmas(STACKS))
                if i % 3 == 0:
                    pe.wait_ge(*pool_qkv.at(seq, f"block{i // 3}"))
                row_bank_free(seq, i + i // 6)
                q, k, dst = q_block[seq.parity], k_stack[seq.parity], row_bank[(i + i // 6) % 2]
                j, kind = divmod(i, 3)
                if kind < 2:
                    for n in range(2):
                        h = G * j + 2 * kind + n
                        mm(dst[:, n * T:(n + 1) * T], q[0:ROWS, h, P:T], k[0:ROWS, h % G, :],
                           start=n == 0, stop=False, skip_group_check=True)
                    mm(dst[:].rearrange("p (a b) -> p a b", a=2)[:, :, P:T], ident_bf[:], row_mask[:, 0:2, :],
                       start=False, stop=True, skip_group_check=True).then_inc(*pe_row.done(f"row{i}"))
                else:
                    for n in range(G):
                        mm(dst[:, n * P:(n + 1) * P], q[0:ROWS, G * j + n, 0:P], k[0:ROWS, n, 0:P],
                           start=n == 0, stop=False, skip_group_check=True)
                    mm(dst[:], ident_bf[:], row_mask[:].rearrange("p a b -> p (a b)"),
                       start=False, stop=True, skip_group_check=True).then_inc(*pe_row.done(f"row{i}"))

            def max_T(seq, half):
                pe.wait_ge(*dve_row.at(seq, f"max{6 * half + 5}"))
                for t in range(NT):
                    last = nc.tensor.transpose(row_bank[half][0:H // 2, t * P:(t + 1) * P],
                                               a_nmax[:, t, half * H // 2:(half + 1) * H // 2], ident[:])
                last.then_inc(*pe_row.done(f"max_T{half}"))

            def col(seq, i):
                if i % 6 == 0:
                    pe.wait_ge(max_moved[i // 6], seq.dmas(1))
                if i >= 2:
                    pe.wait_ge(*act_col.at(seq, f"exp{i - 2}"))
                elif seq.has_before(1):
                    pe.wait_ge(*act_col.at(seq, f"exp{i + 10}", back=1))
                q, k, dst = q_block[seq.parity], k_stack[seq.parity], col_bank[i % 2]
                j, kind = divmod(i, 3)
                if kind < 2:
                    for n in range(2):
                        h = G * j + 2 * kind + n
                        mm(dst[:, n * T:(n + 1) * T], k[0:ROWS + 1, h % G, 0:P], q[0:ROWS + 1, h, :],
                           start=n == 0, stop=False, skip_group_check=True)
                    mm(dst[:].rearrange("p (a b) -> p a b", a=2)[:, :, 0:P], ident_bf[:], col_mask[:, 0:2, :],
                       start=False, stop=True, skip_group_check=True).then_inc(*pe_col.done(f"col{i}"))
                else:
                    for n in range(G):
                        mm(dst[:, n * P:(n + 1) * P], k[0:ROWS + 1, n, P:T], q[0:ROWS + 1, G * j + n, P:T],
                           start=n == 0, stop=False, skip_group_check=True)
                    mm(dst[:], ident_bf[:], col_mask[:].rearrange("p a b -> p (a b)"),
                       start=False, stop=True, skip_group_check=True).then_inc(*pe_col.done(f"col{i}"))

            def pv(seq, j):
                if j == 0:
                    pe.wait_ge(*dve_qkv.at(seq, "v1"))
                    if not seq.has_before(1):
                        pe.wait_ge(act_prep, 5)
                pe.wait_ge(*act_col.at(seq, f"exp{3 * j + 2}"))
                dst, half = pv_bank, (j % 2) * T
                for n in range(G):
                    mm(dst[32 * n:32 * n + 32, half:half + T], v_head[seq.parity][:, 0, G * j + n, :],
                       probs0[j % 2][:, n, :], start=True, stop=False, skip_group_check=True)
                for n in range(G):
                    last = mm(dst[32 * n:32 * n + 32, half + P:half + T], v_head[seq.parity][:, 1, G * j + n, :],
                              probs1[j % 2][:, n, :], start=False, stop=True, skip_group_check=True)
                last.then_inc(*pe_col.done(f"pv{j}"))

            def att_T(seq, t):
                if t == 0:
                    pe.wait_ge(*act_col.at(seq, "out1"))
                    if seq.has_before(1):
                        pe.wait_ge(*dve_proj.at(seq, "y1", back=1))
                else:
                    pe.wait_ge(*dve_proj.at(seq, "o0"))
                transposes(pf_bank, [oT_raw[seq.parity][:, j, t * P:(t + 1) * P] for j in range(G)])\
                    .then_inc(*pe_proj.done(f"att_T{t}"))

            def z_T(seq, proj):
                pe.wait_ge(*dve_mix.at(seq, "z1"))
                if proj:
                    pe.wait_ge(*dve_proj.at(proj, "o1"))
                else:
                    pe.wait_ge(*dve_proj.at(Sequence(B - 1, 1), "y1"))
                    pe.wait_ge(*dve_ffn.at(seq, "u", back=1))
                transposes(pf_bank, [z_ln[:, t, :] for t in range(NT)]).then_inc(*pe_ffn.done("z_T"))

            def o_T(seq, ffn):
                pe.wait_ge(*dve_proj.at(seq, "o1"))
                if ffn:
                    pe.wait_ge(*dve_ffn.at(ffn, "zT_lo"))
                transposes(pf_bank, [o_ln[:, t, :] for t in range(NT)]).then_inc(*pe_proj.done("o_T"))

            def up(seq, half, proj):
                if half == 0:
                    pe.wait_ge(*dve_ffn.at(seq, "zT_lo"))
                if proj:
                    if half == 0:
                        pe.wait_ge(*act_proj.at(proj, "o_T"))
                    else:
                        pe.wait_ge(*act_proj.at(proj, "exp1"))
                elif half == 1:
                    pe.wait_ge(*act_ffn.at(seq, "relu1"))
                for i in range(2):
                    w = W1T[:, (2 * half + i) * P:(2 * half + i + 1) * P]
                    mm(pf_bank[:, i * T:(i + 1) * T], w, zT_hi[:], start=True, stop=False)
                    last = mm(pf_bank[:, i * T:(i + 1) * T], w, zT_lo[:], start=False, stop=True)
                last.then_inc(*pe_ffn.done(f"up{half}"))

            def proj_logits(seq, ffn):
                pe.wait_ge(*act_proj.at(seq, "o_T"))
                if ffn:
                    pe.wait_ge(*act_ffn.at(ffn, "relu1"))
                for t in range(NT):
                    last = mm(pf_bank[:, t * NP:(t + 1) * NP], oT[:, t * P:(t + 1) * P], pKT[:],
                              start=True, stop=True)
                last.then_inc(*pe_proj.done("logits"))

            def proj_prob_T(seq, ffn):
                pe.wait_ge(*act_proj.at(seq, "exp1"))
                if ffn:
                    pe.wait_ge(*act_ffn.at(ffn, "relu3"))
                transposes(pf_bank, [p_exp[:, t, :] for t in range(NT)]).then_inc(*pe_proj.done("prob_T"))

            def down(seq, proj):
                pe.wait_ge(*pool_ffn.at(seq, "lo1"))
                if proj:
                    pe.wait_ge(*dve_proj.at(proj, "prob_T"))
                for t in range(NT):
                    for a in range(FC):
                        for part, hid in enumerate((hidden_hi, hidden_lo)):
                            last = mm(pf_bank[:, t * C:(t + 1) * C], hid[:, a, t * P:(t + 1) * P], W2T[:, a, :],
                                      start=a + part == 0, stop=a == FC - 1 and part == 1)
                last.then_inc(*pe_ffn.done("down"))

            def proj_out(seq, ffn):
                pe.wait_ge(*dve_proj.at(seq, "prob_T"))
                if ffn:
                    pe.wait_ge(*dve_ffn.at(ffn, "u"))
                for t in range(NT):
                    last = mm(pf_bank[:, t * C:(t + 1) * C], pT_exp[:, t * P:(t + 1) * P], pV_sb[:],
                              start=True, stop=True)
                last.then_inc(*pe_proj.done("out"))

            def mix_ln_T(seq):
                pe.wait_ge(*dve_proj.at(seq, "ln1"))
                if seq.has_before(1):
                    pe.wait_ge(*dve_mix.at(seq, "y1", back=1))
                transposes(mix_bank, [f_ln[:, t, :] for t in range(NT)]).then_inc(*pe_mix.done("ln_T"))

            def mix_logits(seq, t):
                if t == 0:
                    pe.wait_ge(*dve_mix.at(seq, "lnT_lo"))
                else:
                    pe.wait_ge(*act_mix.at(seq, "exp0"))
                tok = slice(t * P, (t + 1) * P)
                three_products(mix_bank[:], fT_hi[:, tok], fT_lo[:, tok], fKT_hi[:], fKT_lo[:])\
                    .then_inc(*pe_mix.done(f"logits{t}"))

            def mix_prob_T(seq, t):
                pe.wait_ge(*(act_mix.at(seq, "exp1") if t == 0 else act_mix.at(seq, "prob_T0")))
                transposes(mix_bank, [m_exp[:, t, a * P:(a + 1) * P] for a in range(KC)])\
                    .then_inc(*pe_mix.done(f"prob_T{t}"))

            def mix_out(seq):
                pe.wait_ge(*act_mix.at(seq, "prob_T1"))
                for t in range(NT):
                    for a in range(KC):
                        last = mm(mix_bank[:, t * C:(t + 1) * C], mT_exp[:, t, a, :], fV_sb[:, a, :],
                                  start=a == 0, stop=a == KC - 1)
                last.then_inc(*pe_mix.done("out"))

            def step(qkv, attn, proj, mix, ffn):
                in_order([
                    (row, attn, 0), (mix_ln_T, mix), (att_T, proj, 0), (row, attn, 1), (mix_logits, mix, 0),
                    (att_T, proj, 1), (row, attn, 2), (row, attn, 3), (z_T, ffn, proj), (mix_logits, mix, 1),
                    (qkv_ln_T, qkv), (o_T, proj, ffn), (row, attn, 4), (row, attn, 5), (up, ffn, 0, proj),
                    (qkv_logits, qkv, 0), (mix_prob_T, mix, 0), (max_T, attn, 0), (row, attn, 6),
                    (proj_logits, proj, ffn), (mix_prob_T, mix, 1), (row, attn, 7), (row, attn, 8),
                    (qkv_logits, qkv, 1), (up, ffn, 1, proj), (row, attn, 9), (col, attn, 0), (mix_out, mix),
                    (proj_prob_T, proj, ffn), (col, attn, 1), (col, attn, 2), (qk_prob_T, qkv), (row, attn, 10),
                    (row, attn, 11), (qk, qkv), (col, attn, 3), (down, ffn, proj), (max_T, attn, 1), (col, attn, 4),
                    (pv, attn, 0), (col, attn, 5), (proj_out, proj, ffn), (v_prob_T, qkv), (col, attn, 6),
                    (col, attn, 7), (pv, attn, 1), (col, attn, 8), (v, qkv), (col, attn, 9), (col, attn, 10),
                    (pv, attn, 2), (col, attn, 11), (pv, attn, 3)])

            run_steps(pe, step, prep_rest)


_INS = ["L0_attn_x", "L0_attn_qK", "L0_attn_qV", "L0_attn_kK", "L0_attn_kV", "L0_attn_vK", "L0_attn_vV",
        "L0_attn_pK", "L0_attn_pV", "L0_attn_fK", "L0_attn_fV", "L0_ffn_W1", "L0_ffn_b1", "L0_ffn_W2", "L0_ffn_b2"]


def kernel(**inputs):
    import numpy as _np
    import concourse.bacc as _bacc
    from concourse import mybir as _mybir
    from concourse.bass_utils import run_bass_kernel_spmd as _run

    nc = _bacc.Bacc("TRN2", target_bir_lowering=False, num_devices=1)
    arrays, args = {}, []
    for name in _INS:
        a = _np.ascontiguousarray(inputs[name])
        arrays[f"in_{name}"] = a
        args.append(nc.dram_tensor(f"in_{name}", a.shape, _mybir.dt.from_np(a.dtype), kind="ExternalInput").ap())
    shape = inputs["L0_attn_x"].shape
    out = nc.dram_tensor("out", shape, _mybir.dt.float32, kind="ExternalOutput").ap()
    build_block(nc, *args, out)
    r = _run(nc, [arrays], core_ids=[0])
    return r.results[0]["out"]
```

```python
from contextlib import ExitStack

import concourse.bass as bass
from concourse import mybir

F32 = mybir.dt.float32
F32R = mybir.dt.float32r
BF16 = mybir.dt.bfloat16
ALU = mybir.AluOpType
ACT = mybir.ActivationFunctionType
AX = mybir.AxisListType

P = 128
EPS = 1e-5
MASKED = -1e30
TICKS = 32


class Sequence:

    def __init__(self, number, parity):
        self.number, self.parity = number, parity

    def has_before(self, n):
        return not isinstance(self.number, int) or self.number >= n

    def dmas(self, each, back=0):
        return self.number * (16 * each) + 16 * each * (1 - back)

    def dmas_of_parity(self, back=0):
        return (self.number - self.parity) * 8 + 16 * (1 - back // 2)


class Track:

    def __init__(self, sem, names):
        assert len(names) <= TICKS and len(set(names)) == len(names)
        self.sem, self.names = sem, list(names)

    def done(self, name):
        last = name == self.names[-1]
        return self.sem, TICKS - len(self.names) + 1 if last else 1

    def at(self, seq, name, back=0):
        k = self.names.index(name)
        rise = TICKS if k == len(self.names) - 1 else k + 1
        return self.sem, seq.number * TICKS + (rise - back * TICKS)


def build_block(nc, x, qK, qV, kK, kV, vK, vV, pK, pV, fK, fV, W1, b1, W2, b2, out):
    B, T, C = x.shape
    NP = qK.shape[0]
    NF = fK.shape[0]
    FF = W1.shape[0]
    H = 16
    D = C // H
    NT = T // P
    G = 4
    FC, KC = FF // P, NF // P
    ROWS = 3 * G * D
    SCALE = float(C) ** -0.5
    STAGES = 5
    assert (C, NP, NT, H, D, FC, KC) == (P, P, 2, 16, 8, 4, 4)

    with ExitStack() as ctx:
        def sb(name, shape, dt=F32):
            return ctx.enter_context(nc.sbuf_tensor(name, shape, dt))

        def bank(name):
            return ctx.enter_context(nc.psum_tensor(name, [P, 512], F32))

        def sem(name):
            return ctx.enter_context(nc.semaphore(name))

        def track(name, names):
            return Track(sem(name), names)

        ident = sb("ident", [P, P])
        ident_bf = sb("ident_bf", [P, P], BF16)
        ones = sb("ones", [P, P])
        row_mask = sb("row_mask", [P, G, P], BF16)
        col_mask = sb("col_mask", [P, G, P], BF16)
        block_sel3 = sb("block_sel3", [ROWS, 3, G])
        block_sel = sb("block_sel", [ROWS, G])
        pool_gate = sb("pool_gate", [P, 16])
        dve_gate = sb("dve_gate", [P, 1])
        power = sb("power", [P, 4])
        Kraw = sb("Kraw", [P, 3, C])
        KT_hi = sb("KT_hi", [C, 3 * NP], F32R)
        KT_lo = sb("KT_lo", [C, 3 * NP], F32R)
        Vraw = sb("Vraw", [P, 2, C])
        qkV = sb("qkV", [NP, 2, C])
        vV_sb = sb("vV_sb", [NP, C])
        pK_raw = sb("pK_raw", [NP, C])
        pKT = sb("pKT", [C, NP])
        pV_sb = sb("pV_sb", [NP, C])
        fK_raw = sb("fK_raw", [P, KC, C])
        fKT_hi = sb("fKT_hi", [C, NF], F32R)
        fKT_lo = sb("fKT_lo", [C, NF], F32R)
        fV_sb = sb("fV_sb", [P, KC, C])
        W1_raw = sb("W1_raw", [P, FC, C])
        W2_raw = sb("W2_raw", [C, FF])
        W_neg = sb("W_neg", [P, 512])
        W1_q = sb("W1_q", [P, FC, C])
        W2_q = sb("W2_q", [C, FF])
        W1T = sb("W1T", [C, FF], F32R)
        W2T = sb("W2T", [P, FC, C], F32R)
        W_sums = sb("W_sums", [P, 2])
        W_thr = sb("W_thr", [P, 2])
        W_nthr = sb("W_nthr", [P, 2])
        b_rows = sb("b_rows", [FC + 1, P])
        b_sb = sb("b_sb", [P, FC + 1])

        x_in = [sb(f"x_in{i}", [P, NT, C]) for i in range(2)]
        x1 = [sb(f"x1_{i}", [P, NT, C]) for i in range(2)]
        q_stats = sb("q_stats", [P, NT, 6])
        q_mv = [sb(f"q_mv{i}", [P, NT, 2]) for i in range(2)]
        q_var = sb("q_var", [P, 2, NT])
        q_rstd = [sb(f"q_rstd{i}", [P, 2, NT]) for i in range(2)]
        h_ln = sb("h_ln", [P, NT, C])
        hT_hi = sb("hT_hi", [C, T], F32R)
        hT_lo = sb("hT_lo", [C, T], F32R)
        q_nmax = sb("q_nmax", [P, NT, 3])
        q_sum = sb("q_sum", [P, NT, 3])
        q_rsum = sb("q_rsum", [P, NT, 3])
        q_exp = sb("q_exp", [P, NT, 3, NP])
        q_prob = sb("q_prob", [P, NT, 2, NP])
        qkT_prob = sb("qkT_prob", [NP, 2, T])
        vT_prob = sb("vT_prob", [NP, T])
        qk_hi = sb("qk_hi", [C, 2, T], F32R)
        qk_lo = sb("qk_lo", [C, 2, T], F32R)
        q_stack = sb("q_stack", [ROWS, G, T], F32R)
        k_stack = [sb(f"k_stack{i}", [P, G, T], F32R) for i in range(2)]
        q_block = [sb(f"q_block{i}", [P, H, T], F32R) for i in range(2)]
        v_head = [sb(f"v_head{i}", [P, NT, H, 32]) for i in range(2)]
        a_nmax = sb("a_nmax", [P, NT, H])
        nmaxT = [sb(f"nmaxT{i}", [H // 2, T], F32R) for i in range(2)]
        probs0 = [sb(f"probs0_{i}", [P, G, T]) for i in range(2)]
        probs1 = [sb(f"probs1_{i}", [P, G, P]) for i in range(2)]
        oT_raw = [sb(f"oT_raw{i}", [P, 2, T]) for i in range(2)]
        o_rsum = sb("o_rsum", [P, NT, H])
        o_ln = sb("o_ln", [P, NT, C])
        oT = sb("oT", [C, T])
        p_nmax = sb("p_nmax", [P, NT])
        p_sum = sb("p_sum", [P, NT])
        p_rsum = sb("p_rsum", [P, NT])
        p_exp = sb("p_exp", [P, NT, NP])
        pT_exp = sb("pT_exp", [NP, T])
        y1 = [sb(f"y1_{i}", [P, NT, C]) for i in range(2)]
        p_stats = sb("p_stats", [P, NT, 6])
        p_mv = sb("p_mv", [P, NT, 2])
        p_var = sb("p_var", [P, NT])
        p_rstd = sb("p_rstd", [P, NT])
        f_ln = sb("f_ln", [P, NT, C])
        fT_hi = sb("fT_hi", [C, T], F32R)
        fT_lo = sb("fT_lo", [C, T], F32R)
        m_nmax = sb("m_nmax", [P, NT])
        m_sum = sb("m_sum", [P, NT])
        m_rsum = sb("m_rsum", [P, NT])
        m_exp = sb("m_exp", [P, NT, NF])
        mT_exp = sb("mT_exp", [P, NT, KC, P])
        y2 = sb("y2", [P, NT, C])
        m_stats = sb("m_stats", [P, NT, 6])
        m_mv = sb("m_mv", [P, NT, 2])
        m_var = sb("m_var", [P, NT])
        m_rstd = sb("m_rstd", [P, NT])
        y2_ln = sb("y2_ln", [P, NT, C])
        x_again = sb("x_again", [P, NT, C])
        x2 = [sb(f"x2_{i}", [P, NT, C]) for i in range(2)]
        z_stats = sb("z_stats", [P, NT, 6])
        z_mv = sb("z_mv", [P, NT, 2])
        z_var = sb("z_var", [P, NT])
        z_rstd = sb("z_rstd", [P, NT])
        z_ln = sb("z_ln", [P, NT, C])
        zT_hi = sb("zT_hi", [C, T], F32R)
        zT_lo = sb("zT_lo", [C, T], F32R)
        hidden = sb("hidden", [P, FC, T])
        hidden_hi = sb("hidden_hi", [P, FC, T], F32R)
        hidden_lo = sb("hidden_lo", [P, FC, T], F32R)
        uT = sb("uT", [C, T])
        u_stats = sb("u_stats", [P, NT, 6])
        u_mv = sb("u_mv", [P, NT, 2])
        u_var = sb("u_var", [P, NT])
        u_rstd = sb("u_rstd", [P, NT])
        u_ln = sb("u_ln", [P, NT, C])
        x_out = [sb(f"x_out{i}", [P, NT, C]) for i in range(2)]

        row_bank = [bank(f"row_bank{i}") for i in range(2)]
        col_bank = [bank(f"col_bank{i}") for i in range(2)]
        pv_bank = bank("pv_bank")
        qkv_bank = bank("qkv_bank")
        mix_bank = bank("mix_bank")
        pf_bank = bank("pf_bank")

        pe_qkv = track("pe_qkv", ["ln_T", "logits0", "logits1", "qk_prob_T", "qk", "v_prob_T", "v"])
        dve_qkv = track("dve_qkv", [
            "stats0", "stats1", "mv0", "mv1", "ln0", "ln1", "lnT_lo", "max0", "max1", "rsum0", "rsum1",
            "qk_lo", "v_prob_T", "v0", "v1", "x1_0", "x1_1"])
        act_qkv = track("act_qkv", ["lnT_hi", "exp0q", "exp0k", "exp0v", "exp1q", "exp1k", "exp1v",
                                    "qk_prob_T", "qk_hi"])
        pool_qkv = track("pool_qkv", ["var", "var2", "rstd", "q0", "k0", "q1", "k1",
                                      "block0", "block1", "block2", "block3"])
        pe_row = track("pe_row", [*[f"row{i}" for i in range(6)], "max_T0",
                                  *[f"row{i}" for i in range(6, 12)], "max_T1"])
        dve_row = track("dve_row", [f"max{i}" for i in range(12)])
        act_row = track("act_row", ["max_T0", "max_T1"])
        pe_col = track("pe_col", [*[f"col{i}" for i in range(5)], "pv0", "col5", "col6", "col7", "pv1",
                                  "col8", "col9", "col10", "pv2", "col11", "pv3"])
        act_col = track("act_col", [*[f"exp{i}" for i in range(8)], "out0", *[f"exp{i}" for i in range(8, 12)],
                                    "out1"])
        pe_proj = track("pe_proj", ["att_T", "o_T", "logits", "prob_T", "out"])
        dve_proj = track("dve_proj", ["o_rsum", "o", "max", "prob_T", "rsum", "y0", "y1",
                                      "stats0", "stats1", "mv0", "mv1", "ln0", "ln1"])
        act_proj = track("act_proj", ["o_T", "exp0", "exp1"])
        pool_proj = track("pool_proj", ["var", "rstd"])
        pe_mix = track("pe_mix", ["ln_T", "logits0", "logits1", "prob_T0", "prob_T1", "out"])
        dve_mix = track("dve_mix", ["lnT_lo", "max0", "max1", "rsum", "y0", "y1", "stats0", "stats1",
                                    "mv0", "mv1", "ln0", "ln1", "zstats0", "zstats1", "zmv0", "zmv1",
                                    "z0", "z1"])
        act_mix = track("act_mix", ["lnT_hi", "exp0", "exp1", "prob_T0", "prob_T1"])
        pool_mix = track("pool_mix", ["var", "rstd", "x2", "zvar", "zrstd"])
        pe_ffn = track("pe_ffn", ["z_T", "up0", "up1", "down", "u_T"])
        dve_ffn = track("dve_ffn", ["zT_lo", "u", "stats0", "stats1", "mv0", "mv1", "ln0", "ln1"])
        act_ffn = track("act_ffn", ["zT_hi", "hi0", "relu0", "hi1", "relu1", "hi2", "relu2", "hi3", "relu3"])
        pool_ffn = track("pool_ffn", ["lo0", "lo1", "var", "rstd", "out"])
        x_loaded = [sem(f"x_loaded{i}") for i in range(2)]
        stacked = sem("stacked")
        max_moved = [sem(f"max_moved{i}") for i in range(2)]
        x_reloaded = sem("x_reloaded")
        stored = [sem(f"stored{i}") for i in range(2)]
        K_loads = sem("K_loads")
        V_loads = sem("V_loads")
        late_loads = sem("late_loads")
        consts = sem("consts")
        dve_prep = sem("dve_prep")
        pe_prep = sem("pe_prep")
        act_prep = sem("act_prep")
        STACKS = 6
        CONSTS = 19

        def dram_rows(a, seq):
            flat = a.rearrange("b t c -> (b t) c")
            return flat[bass.ds(seq.number * T, T), :].rearrange("(t p) c -> p t c", p=P)

        def run_steps(eng, step, after_first=None):
            def at(s, number):
                return [Sequence(number - k, (s - k) % 2) if not isinstance(number, int) or 0 <= s - k < B
                        else None for k in range(STAGES)]

            first = STAGES + 1
            for s in range(first):
                step(*at(s, s))
                if s == 0 and after_first:
                    after_first()
            with eng.Fori(first, B - 1, 2) as number:
                step(*at(first, number))
                step(*at(first + 1, number + 1))
            for s in range(B, B + STAGES - 1):
                step(*at(s, s))

        def in_order(pieces):
            for piece, seq, *more in pieces:
                if seq is not None:
                    piece(seq, *more)

        block = ctx.enter_context(nc.Block())

        @block.sync
        def _(sp):
            for i, w in enumerate((qK, kK, vK)):
                sp.dma_start(Kraw[:, i, :], w).then_inc(K_loads, 16)
            def load_x(seq):
                if isinstance(seq.number, int) and seq.number == 0:
                    return
                if seq.has_before(2):
                    sp.wait_ge(*dve_qkv.at(seq, "x1_1", back=2))
                sp.dma_start(x_in[seq.parity][:], dram_rows(x, seq)).then_inc(x_loaded[seq.parity], 16)

            def stack_part(seq, part, q_part, k_part):
                rows = slice(part * G * D, (part + 1) * G * D)
                if q_part is not None:
                    sp.dma_start(q_stack[rows].bitcast(F32), q_part[:, 0, :].bitcast(F32)).then_inc(stacked, 16)
                if k_part is not None:
                    sp.dma_start(k_stack[seq.parity][rows].bitcast(F32),
                                 k_part[:, 1, :].bitcast(F32)).then_inc(stacked, 16)

            def stack_high(seq):
                sp.wait_ge(*act_qkv.at(seq, "qk_hi"))
                if seq.has_before(1):
                    sp.wait_ge(*pool_qkv.at(seq, "block3", back=1))
                if seq.has_before(2):
                    sp.wait_ge(*pe_col.at(seq, "pv3", back=2))
                stack_part(seq, 0, qk_hi, qk_hi)
                stack_part(seq, 1, qk_hi, None)
                stack_part(seq, 2, None, qk_hi)

            def stack_low(seq):
                sp.wait_ge(*dve_qkv.at(seq, "qk_lo"))
                stack_part(seq, 2, qk_lo, None)
                stack_part(seq, 1, None, qk_lo)

            def move_max(seq, half):
                heads = slice(half * H // 2, (half + 1) * H // 2)
                sp.wait_ge(*act_row.at(seq, f"max_T{half}"))
                sp.dma_start(q_block[seq.parity][ROWS:ROWS + 1, heads].bitcast(F32), nmaxT[half][:].bitcast(F32))\
                  .then_inc(max_moved[half], 16)

            def reload_x(seq):
                if seq.has_before(1):
                    sp.wait_ge(*pool_mix.at(seq, "x2", back=1))
                sp.dma_start(x_again[:], dram_rows(x, seq)).then_inc(x_reloaded, 16)

            def store(seq):
                sp.wait_ge(*pool_ffn.at(seq, "out"))
                sp.dma_start(dram_rows(out, seq), x_out[seq.parity][:]).then_inc(stored[seq.parity], 16)

            def step(qkv, attn, proj, mix, ffn):
                in_order([
                    (load_x, qkv), (move_max, attn, 0), (move_max, attn, 1), (stack_high, qkv), (stack_low, qkv),
                    (reload_x, proj), (store, ffn)])

            sp.dma_start(x_in[0][:], dram_rows(x, Sequence(0, 0))).then_inc(x_loaded[0], 16)
            for i, w in enumerate((qV, kV)):
                sp.dma_start(Vraw[:, i, :], w).then_inc(V_loads, 16)
            sp.dma_start(vV_sb[:], vV).then_inc(V_loads, 16)
            for dst, src in ((pK_raw[:], pK), (pV_sb[:], pV),
                             (fK_raw[:], fK.rearrange("(a p) c -> p a c", p=P)),
                             (fV_sb[:], fV.rearrange("(a p) c -> p a c", p=P)),
                             (W1_raw[:], W1.rearrange("(a p) c -> p a c", p=P)),
                             (W2_raw[:], W2),
                             (b_rows[0:FC, :], b1.rearrange("(a p) -> a p", p=P)),
                             (b_rows[FC:FC + 1, :], b2.rearrange("(a c) -> a c", a=1))):
                sp.dma_start(dst, src).then_inc(late_loads, 16)
            run_steps(sp, step)
            for i in range(2):
                sp.wait_ge(stored[i], 16 * B // 2)

        @block.gpsimd
        def _(pool):
            nc.gpsimd.memset(ident[:], 0.0).then_inc(consts, 1)
            pool.wait_ge(consts, 1)
            nc.gpsimd.affine_select(out=ident[:], in_=ident[:], compare_op=ALU.not_equal, fill=1.0, base=0,
                                    pattern=[[-1, P]], channel_multiplier=1).then_inc(consts, 1)
            nc.gpsimd.memset(block_sel3[:], 1.0).then_inc(consts, 1)
            nc.gpsimd.memset(ident_bf[:], 0.0).then_inc(consts, 1)
            nc.gpsimd.memset(power[:], -0.5).then_inc(consts, 1)
            nc.gpsimd.memset(row_mask[:], 0.0).then_inc(consts, 1)
            nc.gpsimd.memset(col_mask[:], 0.0).then_inc(consts, 1)
            nc.gpsimd.memset(ones[:], 1.0).then_inc(consts, 1)
            pool.wait_ge(consts, 8)
            nc.gpsimd.affine_select(out=block_sel3[:], in_=block_sel3[:], compare_op=ALU.is_ge, fill=0.0,
                                    base=0, pattern=[[-G * D, 3], [-D, G]], channel_multiplier=1)\
                .then_inc(consts, 1)
            nc.gpsimd.affine_select(out=ident_bf[:], in_=ident_bf[:], compare_op=ALU.not_equal, fill=1.0,
                                    base=0, pattern=[[-1, P]], channel_multiplier=1).then_inc(consts, 1)
            nc.gpsimd.affine_select(out=row_mask[:], in_=row_mask[:], compare_op=ALU.is_ge, fill=MASKED,
                                    base=0, pattern=[[0, G], [-1, P]], channel_multiplier=1).then_inc(consts, 1)
            nc.gpsimd.affine_select(out=col_mask[:], in_=col_mask[:], compare_op=ALU.is_ge, fill=MASKED,
                                    base=0, pattern=[[0, G], [1, P]], channel_multiplier=-1).then_inc(consts, 1)
            pool.wait_ge(consts, 12)
            nc.gpsimd.affine_select(out=block_sel3[:], in_=block_sel3[:], compare_op=ALU.is_ge, fill=0.0,
                                    base=D - 1, pattern=[[G * D, 3], [D, G]], channel_multiplier=-1)\
                .then_inc(consts, 1)
            for i in range(2):
                nc.gpsimd.memset(v_head[i][:], 0.0).then_inc(consts, 1)
            pool.wait_ge(consts, 15)
            for i in range(2):
                nc.gpsimd.memset(k_stack[i][ROWS:ROWS + 1, :, :].bitcast(F32), 1.0).then_inc(consts, 1)
            pool.wait_ge(consts, 17)
            for i in range(2):
                nc.gpsimd.memset(v_head[i][:, :, :, D:D + 1], 1.0).then_inc(consts, 1)

            gates = iter(range(1000))

            def gate():
                n = next(gates) % pool_gate.shape[1]
                nc.gpsimd.tensor_tensor(pool_gate[:, n:n + 1], power[:, 0:1], power[:, 0:1], ALU.mult)

            def qkv_rstd(seq):
                pool.wait_ge(*dve_qkv.at(seq, "mv1"))
                gate()
                mv = q_mv[seq.parity]
                nc.gpsimd.tensor_scalar(q_var[:, 0, :], mv[:, :, 1], 1.0, EPS, ALU.mult, ALU.add)\
                    .then_inc(*pool_qkv.done("var"))
                nc.gpsimd.tensor_scalar(q_var[:, 1, :], mv[:, :, 1], 1.0 + EPS, EPS * EPS, ALU.mult, ALU.add)\
                    .then_inc(*pool_qkv.done("var2"))
                pool.wait_ge(*pool_qkv.at(seq, "var2"))
                if seq.has_before(2):
                    pool.wait_ge(*dve_qkv.at(seq, "x1_1", back=2))
                nc.gpsimd.tensor_tensor(q_rstd[seq.parity][:].rearrange("p a b -> p (a b)"),
                                        q_var[:].rearrange("p a b -> p (a b)"), power[:, 0:4], ALU.pow)\
                    .then_inc(*pool_qkv.done("rstd"))

            def qk_probs(seq, t):
                pool.wait_ge(*dve_qkv.at(seq, f"rsum{t}"))
                if seq.has_before(1):
                    pool.wait_ge(*pe_qkv.at(seq, "qk_prob_T", back=1))
                gate()
                for i, which in enumerate("qk"):
                    nc.gpsimd.tensor_scalar(q_prob[:, t, i, :], q_exp[:, t, i, :], q_rsum[:, t, i:i + 1], 1.0,
                                            ALU.mult, ALU.mult).then_inc(*pool_qkv.done(f"{which}{t}"))

            def q_blocks(seq, j):
                if j == 0:
                    pool.wait_ge(stacked, seq.dmas(STACKS))
                    if seq.has_before(2):
                        pool.wait_ge(*pe_col.at(seq, "pv3", back=2))
                    gate()
                nc.gpsimd.tensor_scalar(q_block[seq.parity][0:ROWS, G * j:G * j + G, :],
                                        q_stack[:].bitcast(F32), block_sel[:, j:j + 1], 1.0,
                                        ALU.mult, ALU.mult).then_inc(*pool_qkv.done(f"block{j}"))

            def rstd(seq, stage, var_of, names, mv, var, out_, readers):
                pool.wait_ge(*var_of)
                if readers:
                    pool.wait_ge(*readers)
                gate()
                nc.gpsimd.tensor_scalar(var[:], mv[:, :, 1], 1.0, EPS, ALU.mult, ALU.add)\
                    .then_inc(*stage.done(names[0]))
                pool.wait_ge(*stage.at(seq, names[0]))
                nc.gpsimd.tensor_tensor(out_[:], var[:], power[:, 0:NT], ALU.pow).then_inc(*stage.done(names[1]))

            def proj_rstd(seq):
                rstd(seq, pool_proj, dve_proj.at(seq, "mv1"), ("var", "rstd"), p_mv, p_var, p_rstd, None)

            def mix_rstd(seq):
                rstd(seq, pool_mix, dve_mix.at(seq, "mv1"), ("var", "rstd"), m_mv, m_var, m_rstd, None)

            def add_x2(seq):
                pool.wait_ge(*dve_mix.at(seq, "ln1"))
                pool.wait_ge(x_reloaded, seq.dmas(1))
                if seq.has_before(2):
                    pool.wait_ge(*pool_ffn.at(seq, "out", back=2))
                nc.gpsimd.tensor_tensor(x2[seq.parity][:], y2_ln[:], x_again[:], ALU.add)\
                    .then_inc(*pool_mix.done("x2"))

            def z_rstd_(seq):
                rstd(seq, pool_mix, dve_mix.at(seq, "zmv1"), ("zvar", "zrstd"), z_mv, z_var, z_rstd, None)

            def hidden_low(seq, half):
                pool.wait_ge(*act_ffn.at(seq, f"relu{2 * half + 1}"))
                if seq.has_before(1):
                    pool.wait_ge(*pe_ffn.at(seq, "down", back=1))
                part = slice(2 * half, 2 * half + 2)
                nc.gpsimd.tensor_tensor(hidden_lo[:, part, :], hidden[:, part, :], hidden_hi[:, part, :].bitcast(F32),
                                        ALU.subtract).then_inc(*pool_ffn.done(f"lo{half}"))

            def ffn_rstd(seq):
                rstd(seq, pool_ffn, dve_ffn.at(seq, "mv1"), ("var", "rstd"), u_mv, u_var, u_rstd, None)

            def add_out(seq):
                pool.wait_ge(*dve_ffn.at(seq, "ln1"))
                if seq.has_before(2):
                    pool.wait_ge(stored[seq.parity], seq.dmas_of_parity(back=2))
                nc.gpsimd.tensor_tensor(x_out[seq.parity][:], u_ln[:], x2[seq.parity][:], ALU.add)\
                    .then_inc(*pool_ffn.done("out"))

            def step(qkv, attn, proj, mix, ffn):
                in_order([
                    (q_blocks, attn, 2), (q_blocks, attn, 3), (qkv_rstd, qkv), (hidden_low, ffn, 0),
                    (qk_probs, qkv, 0), (qk_probs, qkv, 1), (hidden_low, ffn, 1), (mix_rstd, mix), (add_x2, mix),
                    (ffn_rstd, ffn), (proj_rstd, proj), (z_rstd_, mix), (add_out, ffn), (q_blocks, qkv, 0),
                    (q_blocks, qkv, 1)])

            run_steps(pool, step)

        @block.scalar
        def _(act):
            def copy(dst, src, scale=1.0):
                return nc.scalar.activation(dst, src, ACT.Copy, scale=scale)

            act.wait_ge(pe_prep, 1)
            copy(KT_hi[:], qkv_bank[:, 0:3 * NP], scale=SCALE).then_inc(act_prep, 1)

            def prep_rest():
                act.wait_ge(pe_prep, 2)
                copy(fKT_hi[:], mix_bank[:], scale=SCALE).then_inc(act_prep, 1)
                act.wait_ge(pe_prep, 3)
                copy(pKT[:], pf_bank[:, 0:NP], scale=SCALE).then_inc(act_prep, 1)
                act.wait_ge(dve_prep, 7)
                act.wait_ge(pe_prep, 5)
                copy(W1T[:], mix_bank[:]).then_inc(act_prep, 1)
                act.wait_ge(pe_prep, 6)
                copy(W2T[:].rearrange("p a c -> p (a c)"), pv_bank[:]).then_inc(act_prep, 1)

            def qkv_lnT(seq):
                act.wait_ge(*pe_qkv.at(seq, "ln_T"))
                copy(hT_hi[:], qkv_bank[:, 0:T]).then_inc(*act_qkv.done("lnT_hi"))

            def qkv_exp(seq, t):
                act.wait_ge(*dve_qkv.at(seq, f"max{t}"))
                if seq.has_before(1):
                    act.wait_ge(*pool_qkv.at(seq, f"k{t}", back=1))
                    act.wait_ge(*pe_qkv.at(seq, "v_prob_T", back=1))
                for i, which in enumerate("qkv"):
                    nc.scalar.activation(q_exp[:, t, i, :], qkv_bank[:, i * NP:(i + 1) * NP], ACT.Exp,
                                         bias=q_nmax[:, t, i:i + 1], accum_out=q_sum[:, t, i:i + 1])\
                      .then_inc(*act_qkv.done(f"exp{t}{which}"))

            def qk_prob_T(seq):
                act.wait_ge(*pe_qkv.at(seq, "qk_prob_T"))
                copy(qkT_prob[:].rearrange("p a b -> p (a b)"), qkv_bank[:]).then_inc(*act_qkv.done("qk_prob_T"))

            def qk_high(seq):
                act.wait_ge(*pe_qkv.at(seq, "qk"))
                if seq.has_before(1):
                    act.wait_ge(stacked, seq.dmas(STACKS, back=1))
                copy(qk_hi[:].rearrange("p a b -> p (a b)"), qkv_bank[:]).then_inc(*act_qkv.done("qk_hi"))

            def max_T(seq, half):
                act.wait_ge(*pe_row.at(seq, f"max_T{half}"))
                if seq.has_before(1):
                    act.wait_ge(max_moved[half], seq.dmas(1, back=1))
                copy(nmaxT[half][:], row_bank[half][0:H // 2, 0:T]).then_inc(*act_row.done(f"max_T{half}"))

            def attn_exp(seq, i):
                act.wait_ge(*pe_col.at(seq, f"col{i}"))
                j, kind = divmod(i, 3)
                src = col_bank[i % 2]
                if kind < 2:
                    dst = probs0[j % 2][:, 2 * kind:2 * kind + 2, :].rearrange("p a b -> p (a b)")
                else:
                    dst = probs1[j % 2][:].rearrange("p a b -> p (a b)")
                nc.scalar.activation(dst, src[:], ACT.Exp).then_inc(*act_col.done(f"exp{i}"))

            def attn_out(seq, half):
                act.wait_ge(*pe_col.at(seq, f"pv{2 * half + 1}"))
                if seq.has_before(2):
                    act.wait_ge(*pe_proj.at(seq, "att_T", back=2))
                copy(oT_raw[seq.parity][:, half, :], pv_bank[:, half * T:(half + 1) * T])\
                    .then_inc(*act_col.done(f"out{half}"))

            def proj_o_T(seq):
                act.wait_ge(*pe_proj.at(seq, "o_T"))
                copy(oT[:], pf_bank[:, 0:T]).then_inc(*act_proj.done("o_T"))

            def proj_exp(seq):
                act.wait_ge(*dve_proj.at(seq, "max"))
                if seq.has_before(1):
                    act.wait_ge(*pe_proj.at(seq, "prob_T", back=1))
                for t in range(NT):
                    nc.scalar.activation(p_exp[:, t, :], pf_bank[:, t * NP:(t + 1) * NP], ACT.Exp,
                                         bias=p_nmax[:, t:t + 1], accum_out=p_sum[:, t:t + 1])\
                      .then_inc(*act_proj.done(f"exp{t}"))

            def mix_lnT(seq):
                act.wait_ge(*pe_mix.at(seq, "ln_T"))
                copy(fT_hi[:], mix_bank[:, 0:T]).then_inc(*act_mix.done("lnT_hi"))

            def mix_exp(seq, t):
                act.wait_ge(*dve_mix.at(seq, f"max{t}"))
                if seq.has_before(1):
                    act.wait_ge(*pe_mix.at(seq, f"prob_T{t}", back=1))
                nc.scalar.activation(m_exp[:, t, :], mix_bank[:], ACT.Exp, bias=m_nmax[:, t:t + 1],
                                     accum_out=m_sum[:, t:t + 1]).then_inc(*act_mix.done(f"exp{t}"))

            def mix_prob_T(seq, t):
                act.wait_ge(*pe_mix.at(seq, f"prob_T{t}"))
                copy(mT_exp[:, t].rearrange("p a b -> p (a b)"), mix_bank[:]).then_inc(*act_mix.done(f"prob_T{t}"))

            def ffn_zT(seq):
                act.wait_ge(*pe_ffn.at(seq, "z_T"))
                copy(zT_hi[:], pf_bank[:, 0:T]).then_inc(*act_ffn.done("zT_hi"))

            def ffn_relu(seq, half):
                act.wait_ge(*pe_ffn.at(seq, f"up{half}"))
                if seq.has_before(1):
                    act.wait_ge(*pool_ffn.at(seq, f"lo{half}", back=1))
                    act.wait_ge(*pe_ffn.at(seq, "down", back=1))
                for i in range(2):
                    a = 2 * half + i
                    nc.scalar.activation(hidden_hi[:, a, :], pf_bank[:, i * T:(i + 1) * T], ACT.Relu,
                                         bias=b_sb[:, a:a + 1]).then_inc(*act_ffn.done(f"hi{a}"))
                    nc.scalar.activation(hidden[:, a, :], pf_bank[:, i * T:(i + 1) * T], ACT.Relu,
                                         bias=b_sb[:, a:a + 1]).then_inc(*act_ffn.done(f"relu{a}"))

            def step(qkv, attn, proj, mix, ffn):
                in_order([
                    (attn_out, proj, 0), (mix_lnT, mix), (attn_exp, proj, 9), (attn_exp, proj, 10),
                    (attn_exp, proj, 11), (attn_out, proj, 1), (mix_exp, mix, 0), (ffn_zT, ffn), (proj_o_T, proj),
                    (qkv_lnT, qkv), (mix_exp, mix, 1), (ffn_relu, ffn, 0), (mix_prob_T, mix, 0), (max_T, attn, 0),
                    (qkv_exp, qkv, 0), (proj_exp, proj), (mix_prob_T, mix, 1), (qkv_exp, qkv, 1), (ffn_relu, ffn, 1),
                    (attn_exp, attn, 0), (qk_prob_T, qkv), (attn_exp, attn, 1), (max_T, attn, 1),
                    (attn_exp, attn, 2), (qk_high, qkv), (attn_exp, attn, 3), (attn_exp, attn, 4),
                    (attn_exp, attn, 5), (attn_exp, attn, 6), (attn_exp, attn, 7), (attn_exp, attn, 8)])

            run_steps(act, step, prep_rest)

        @block.vector
        def _(dve):
            def flat(ap):
                return ap.rearrange("p a b -> p (a b)")

            dve.wait_ge(act_prep, 1)
            nc.vector.scalar_tensor_tensor(KT_lo[:], qkv_bank[:, 0:3 * NP], SCALE, KT_hi[:].bitcast(F32),
                                           ALU.mult, ALU.subtract).then_inc(dve_prep, 1)
            dve.wait_ge(V_loads, 16 * 3)
            for i, scale in enumerate((float(D) ** -0.5, 1.0)):
                for half in range(2):
                    for pair in range(2):
                        stacked_order = qkV[:, i, half * C // 2:(half + 1) * C // 2]\
                            .rearrange("p (j d g) -> p g j d", j=2, d=D, g=G)[:, 2 * pair:2 * pair + 2]
                        heads = Vraw[:, i, half * C // 2:(half + 1) * C // 2]\
                            .rearrange("p (g j r d) -> p g j r d", g=2, j=2, r=2, d=D)[:, :, :, pair, :]
                        last = nc.vector.tensor_scalar(stacked_order, heads, scale, None, ALU.mult)
                last.then_inc(dve_prep, 1)
            dve.wait_ge(consts, CONSTS)
            nc.vector.tensor_reduce(block_sel[:], block_sel3[:].rearrange("p a b -> p b a"), axis=AX.X,
                                    op=ALU.add).then_inc(dve_prep, 1)

            def prep_rest():
                dve.wait_ge(late_loads, 16 * 8)
                nc.vector.tensor_reduce(W_sums[:, 0:1], flat(W1_raw[:]), axis=AX.X, op=ALU.add,
                                        apply_absolute_value=True).then_inc(dve_prep, 1)
                nc.vector.tensor_reduce(W_sums[:, 1:2], W2_raw[:], axis=AX.X, op=ALU.add,
                                        apply_absolute_value=True).then_inc(dve_prep, 1)
                dve.wait_ge(act_prep, 2)
                nc.vector.scalar_tensor_tensor(fKT_lo[:], mix_bank[:], SCALE, fKT_hi[:].bitcast(F32),
                                               ALU.mult, ALU.subtract).then_inc(dve_prep, 1)
                dve.wait_ge(act_prep, 3)
                dve.wait_ge(pe_prep, 4)
                nc.vector.tensor_scalar(W_thr[:], pf_bank[:, 0:2], 0.5 / (FF * C), 0.5 * EPS, ALU.mult, ALU.add)\
                  .then_inc(dve_prep, 1)
                dve.wait_ge(dve_prep, 8)
                nc.vector.tensor_scalar(W_nthr[:], W_thr[:], -1.0, None, ALU.mult).then_inc(dve_prep, 1)
                nc.vector.tensor_copy(b_sb[:], pf_bank[:, P:P + FC + 1]).then_inc(dve_prep, 1)
                dve.wait_ge(dve_prep, 9)
                nc.vector.tensor_scalar(W_neg[:], flat(W1_raw[:]), W_nthr[:, 0:1], None, ALU.is_lt)\
                  .then_inc(dve_prep, 1)
                dve.wait_ge(dve_prep, 11)
                nc.vector.scalar_tensor_tensor(flat(W1_q[:]), flat(W1_raw[:]), W_thr[:, 0:1], W_neg[:],
                                               ALU.is_gt, ALU.subtract).then_inc(dve_prep, 1)
                dve.wait_ge(dve_prep, 12)
                nc.vector.tensor_scalar(W_neg[:], W2_raw[:], W_nthr[:, 1:2], None, ALU.is_lt)\
                  .then_inc(dve_prep, 1)
                dve.wait_ge(dve_prep, 13)
                nc.vector.scalar_tensor_tensor(W2_q[:], W2_raw[:], W_thr[:, 1:2], W_neg[:],
                                               ALU.is_gt, ALU.subtract).then_inc(dve_prep, 1)

            def norm_stats(seq, src, stats, mv, stage, prefix=""):
                for t in range(NT):
                    nc.vector.bn_stats(stats[:, t, :], src[:, t, :]).then_inc(*stage.done(f"{prefix}stats{t}"))
                dve.wait_ge(*stage.at(seq, f"{prefix}stats{NT - 1}"))
                nc.vector.memset(dve_gate[:], 0.0)
                for t in range(NT):
                    nc.vector.bn_aggr(mv[:, t, :], stats[:, t, :]).then_inc(*stage.done(f"{prefix}mv{t}"))

            def normalise(dst, src, mv, rstd, t):
                return nc.vector.tensor_scalar(dst, src, mv[:, t, 0:1], rstd[:, t:t + 1], ALU.subtract, ALU.mult)

            def qkv_stats(seq):
                dve.wait_ge(x_loaded[seq.parity], seq.dmas_of_parity())
                norm_stats(seq, x_in[seq.parity], q_stats, q_mv[seq.parity], dve_qkv)

            def qkv_ln(seq):
                dve.wait_ge(*pool_qkv.at(seq, "rstd"))
                if seq.has_before(1):
                    dve.wait_ge(*pe_qkv.at(seq, "ln_T", back=1))
                for t in range(NT):
                    normalise(h_ln[:, t, :], x_in[seq.parity][:, t, :], q_mv[seq.parity],
                              q_rstd[seq.parity][:, 1, :], t).then_inc(*dve_qkv.done(f"ln{t}"))

            def qkv_lnT(seq):
                dve.wait_ge(*act_qkv.at(seq, "lnT_hi"))
                if seq.has_before(1):
                    dve.wait_ge(*pe_qkv.at(seq, "logits1", back=1))
                nc.vector.tensor_tensor(hT_lo[:], qkv_bank[:, 0:T], hT_hi[:].bitcast(F32), ALU.subtract)\
                  .then_inc(*dve_qkv.done("lnT_lo"))

            def qkv_max(seq, t):
                dve.wait_ge(*pe_qkv.at(seq, f"logits{t}"))
                nc.vector.tensor_reduce(q_nmax[:, t, :], qkv_bank[:, 0:3 * NP].rearrange("p (a b) -> p a b", a=3),
                                        axis=AX.X, op=ALU.max, negate=True).then_inc(*dve_qkv.done(f"max{t}"))

            def qkv_rsum(seq, t):
                dve.wait_ge(*act_qkv.at(seq, f"exp{t}v"))
                nc.vector.reciprocal(q_rsum[:, t, :], q_sum[:, t, :]).then_inc(*dve_qkv.done(f"rsum{t}"))

            def qk_low(seq):
                dve.wait_ge(*act_qkv.at(seq, "qk_hi"))
                nc.vector.tensor_tensor(flat(qk_lo[:]), qkv_bank[:], flat(qk_hi[:]).bitcast(F32), ALU.subtract)\
                  .then_inc(*dve_qkv.done("qk_lo"))

            def v_prob_T(seq):
                dve.wait_ge(*pe_qkv.at(seq, "v_prob_T"))
                nc.vector.tensor_copy(vT_prob[:], qkv_bank[:, 0:T]).then_inc(*dve_qkv.done("v_prob_T"))

            def v_out(seq):
                dve.wait_ge(*pe_qkv.at(seq, "v"))
                if seq.has_before(2):
                    dve.wait_ge(*pe_col.at(seq, "pv3", back=2))
                for t in range(NT):
                    nc.vector.tensor_scalar(v_head[seq.parity][:, t, :, 0:D],
                                            qkv_bank[:, t * P:(t + 1) * P].rearrange("p (h d) -> p h d", d=D),
                                            q_rsum[:, t, 2:3], None, ALU.mult).then_inc(*dve_qkv.done(f"v{t}"))

            def keep_x1(seq):
                for t in range(NT):
                    normalise(x1[seq.parity][:, t, :], x_in[seq.parity][:, t, :], q_mv[seq.parity],
                              q_rstd[seq.parity][:, 0, :], t).then_inc(*dve_qkv.done(f"x1_{t}"))

            def attn_max(seq, i):
                dve.wait_ge(*pe_row.at(seq, f"row{i}"))
                j, kind = divmod(i, 3)
                src = row_bank[(i + i // 6) % 2]
                if kind < 2:
                    h = G * j + 2 * kind
                    nc.vector.tensor_reduce(a_nmax[:, 1, h:h + 2], src[:].rearrange("p (a b) -> p a b", a=2),
                                            axis=AX.X, op=ALU.max, negate=True).then_inc(*dve_row.done(f"max{i}"))
                else:
                    nc.vector.tensor_reduce(a_nmax[:, 0, G * j:G * j + G], src[:].rearrange("p (a b) -> p a b", a=G),
                                            axis=AX.X, op=ALU.max, negate=True).then_inc(*dve_row.done(f"max{i}"))

            def proj_o(seq):
                dve.wait_ge(*pe_proj.at(seq, "att_T"))
                heads = pf_bank[:].rearrange("p (h r) -> p h r", r=16)
                nc.vector.reciprocal(flat(o_rsum[:]), heads[:, :, D]).then_inc(*dve_proj.done("o_rsum"))
                dve.wait_ge(*dve_proj.at(seq, "o_rsum"))
                nc.vector.tensor_tensor(flat(o_ln[:]).rearrange("p (h d) -> p h d", d=D), heads[:, :, 0:D],
                                        flat(o_rsum[:]).unsqueeze(2).broadcast_to([P, NT * H, D]), ALU.mult)\
                  .then_inc(*dve_proj.done("o"))

            def proj_max(seq):
                dve.wait_ge(*pe_proj.at(seq, "logits"))
                nc.vector.tensor_reduce(p_nmax[:], pf_bank[:, 0:T].rearrange("p (a b) -> p a b", a=NT),
                                        axis=AX.X, op=ALU.max, negate=True).then_inc(*dve_proj.done("max"))

            def proj_prob_T(seq):
                dve.wait_ge(*pe_proj.at(seq, "prob_T"))
                nc.vector.tensor_copy(pT_exp[:], pf_bank[:, 0:T]).then_inc(*dve_proj.done("prob_T"))

            def residual(seq, stage, src, rsum, sums, add, dst):
                nc.vector.reciprocal(rsum[:], sums[:]).then_inc(*stage.done("rsum"))
                dve.wait_ge(*stage.at(seq, "rsum"))
                for t in range(NT):
                    nc.vector.scalar_tensor_tensor(dst[:, t, :], src[:, t * P:(t + 1) * P], rsum[:, t:t + 1],
                                                   add[:, t, :], ALU.mult, ALU.add).then_inc(*stage.done(f"y{t}"))

            def proj_y1(seq):
                dve.wait_ge(*pe_proj.at(seq, "out"))
                dve.wait_ge(*dve_qkv.at(seq, "x1_1"))
                residual(seq, dve_proj, pf_bank, p_rsum, p_sum, x1[seq.parity], y1[seq.parity])

            def proj_stats(seq):
                dve.wait_ge(*dve_proj.at(seq, "y1"))
                norm_stats(seq, y1[seq.parity], p_stats, p_mv, dve_proj)

            def proj_ln(seq):
                dve.wait_ge(*pool_proj.at(seq, "rstd"))
                if seq.has_before(1):
                    dve.wait_ge(*pe_mix.at(seq, "ln_T", back=1))
                for t in range(NT):
                    normalise(f_ln[:, t, :], y1[seq.parity][:, t, :], p_mv, p_rstd, t)\
                        .then_inc(*dve_proj.done(f"ln{t}"))

            def mix_lnT(seq):
                dve.wait_ge(*act_mix.at(seq, "lnT_hi"))
                nc.vector.tensor_tensor(fT_lo[:], mix_bank[:, 0:T], fT_hi[:].bitcast(F32), ALU.subtract)\
                  .then_inc(*dve_mix.done("lnT_lo"))

            def mix_max(seq, t):
                dve.wait_ge(*pe_mix.at(seq, f"logits{t}"))
                nc.vector.tensor_reduce(m_nmax[:, t:t + 1], mix_bank[:], axis=AX.X, op=ALU.max, negate=True)\
                  .then_inc(*dve_mix.done(f"max{t}"))

            def mix_y2(seq):
                dve.wait_ge(*pe_mix.at(seq, "out"))
                residual(seq, dve_mix, mix_bank, m_rsum, m_sum, y1[seq.parity], y2)

            def mix_stats(seq):
                dve.wait_ge(*dve_mix.at(seq, "y1"))
                norm_stats(seq, y2, m_stats, m_mv, dve_mix)

            def mix_ln(seq):
                dve.wait_ge(*pool_mix.at(seq, "rstd"))
                if seq.has_before(1):
                    dve.wait_ge(*pool_mix.at(seq, "x2", back=1))
                for t in range(NT):
                    normalise(y2_ln[:, t, :], y2[:, t, :], m_mv, m_rstd, t).then_inc(*dve_mix.done(f"ln{t}"))

            def z_stats_(seq):
                dve.wait_ge(*pool_mix.at(seq, "x2"))
                norm_stats(seq, x2[seq.parity], z_stats, z_mv, dve_mix, "z")

            def z_norm(seq):
                dve.wait_ge(*pool_mix.at(seq, "zrstd"))
                if seq.has_before(1):
                    dve.wait_ge(*pe_ffn.at(seq, "z_T", back=1))
                for t in range(NT):
                    normalise(z_ln[:, t, :], x2[seq.parity][:, t, :], z_mv, z_rstd, t)\
                        .then_inc(*dve_mix.done(f"z{t}"))

            def ffn_zT(seq):
                dve.wait_ge(*act_ffn.at(seq, "zT_hi"))
                nc.vector.tensor_tensor(zT_lo[:], pf_bank[:, 0:T], zT_hi[:].bitcast(F32), ALU.subtract)\
                  .then_inc(*dve_ffn.done("zT_lo"))

            def ffn_u(seq):
                dve.wait_ge(*pe_ffn.at(seq, "down"))
                nc.vector.tensor_scalar(uT[:], pf_bank[:, 0:T], b_sb[:, FC:FC + 1], None, ALU.add)\
                  .then_inc(*dve_ffn.done("u"))

            u = mix_bank[:, 0:NT * C].rearrange("p (t c) -> p t c", t=NT)

            def ffn_stats(seq):
                dve.wait_ge(*pe_ffn.at(seq, "u_T"))
                norm_stats(seq, u, u_stats, u_mv, dve_ffn)

            def ffn_ln(seq):
                dve.wait_ge(*pool_ffn.at(seq, "rstd"))
                if seq.has_before(1):
                    dve.wait_ge(*pool_ffn.at(seq, "out", back=1))
                for t in range(NT):
                    normalise(u_ln[:, t, :], u[:, t, :], u_mv, u_rstd, t).then_inc(*dve_ffn.done(f"ln{t}"))

            def step(qkv, attn, proj, mix, ffn):
                in_order([
                    (qkv_stats, qkv), (attn_max, attn, 0), (proj_o, proj), (attn_max, attn, 1), (attn_max, attn, 2),
                    (ffn_zT, ffn), (qkv_ln, qkv), (mix_max, mix, 1), (attn_max, attn, 3), (attn_max, attn, 4),
                    (qkv_lnT, qkv), (attn_max, attn, 5), (qkv_max, qkv, 0), (attn_max, attn, 6), (proj_max, proj),
                    (attn_max, attn, 7), (attn_max, attn, 8), (qkv_max, qkv, 1), (qkv_rsum, qkv, 0),
                    (attn_max, attn, 9), (qkv_rsum, qkv, 1), (mix_y2, mix), (mix_stats, mix), (proj_prob_T, proj),
                    (attn_max, attn, 10), (attn_max, attn, 11), (ffn_u, ffn), (mix_ln, mix), (ffn_stats, ffn),
                    (proj_y1, proj), (qk_low, qkv), (proj_stats, proj), (v_prob_T, qkv), (z_stats_, mix),
                    (ffn_ln, ffn), (proj_ln, proj), (v_out, qkv), (keep_x1, qkv), (z_norm, mix), (mix_lnT, proj),
                    (mix_max, proj, 0)])

            run_steps(dve, step, prep_rest)

        @block.tensor
        def _(pe):
            mm = nc.tensor.matmul

            pe.wait_ge(consts, 2)
            pe.wait_ge(K_loads, 16 * 3)
            for i in range(3):
                last = nc.tensor.transpose(qkv_bank[:, i * NP:(i + 1) * NP], Kraw[:, i, :], ident[:])
            last.then_inc(pe_prep, 1)

            def prep_rest():
                pe.wait_ge(consts, CONSTS)
                pe.wait_ge(late_loads, 16 * 8)
                for a in range(KC):
                    last = nc.tensor.transpose(mix_bank[:, a * P:(a + 1) * P], fK_raw[:, a, :], ident[:])
                last.then_inc(pe_prep, 1)
                nc.tensor.transpose(pf_bank[:, 0:NP], pK_raw[:], ident[:]).then_inc(pe_prep, 1)
                pe.wait_ge(act_prep, 3)
                pe.wait_ge(dve_prep, 6)
                mm(pf_bank[:, 0:2], ones[:], W_sums[:], start=True, stop=True)
                nc.tensor.transpose(pf_bank[:, P:P + FC + 1], b_rows[:], ident[0:FC + 1, 0:FC + 1])\
                    .then_inc(pe_prep, 1)
                pe.wait_ge(dve_prep, 14)
                for a in range(FC):
                    last = nc.tensor.transpose(mix_bank[:, a * P:(a + 1) * P], W1_q[:, a, :], ident[:])
                last.then_inc(pe_prep, 1)
                for a in range(FC):
                    last = nc.tensor.transpose(pv_bank[:, a * P:(a + 1) * P], W2_q[:, a * P:(a + 1) * P], ident[:])
                last.then_inc(pe_prep, 1)

            def transposes(bank_, srcs):
                for i, src in enumerate(srcs):
                    last = nc.tensor.transpose(bank_[:, i * P:(i + 1) * P], src, ident[:])
                return last

            def three_products(out_, hi, lo, w_hi, w_lo):
                mm(out_, hi, w_hi, start=True, stop=False)
                mm(out_, hi, w_lo, start=False, stop=False)
                return mm(out_, lo, w_hi, start=False, stop=True)

            def qkv_ln_T(seq):
                pe.wait_ge(*dve_qkv.at(seq, "ln1"))
                if seq.has_before(1):
                    pe.wait_ge(*dve_qkv.at(seq, "v1", back=1))
                else:
                    pe.wait_ge(dve_prep, 4)
                transposes(qkv_bank, [h_ln[:, t, :] for t in range(NT)]).then_inc(*pe_qkv.done("ln_T"))

            def qkv_logits(seq, t):
                if t == 0:
                    pe.wait_ge(*dve_qkv.at(seq, "lnT_lo"))
                else:
                    pe.wait_ge(*act_qkv.at(seq, f"exp{t - 1}v"))
                tok = slice(t * P, (t + 1) * P)
                three_products(qkv_bank[:, 0:3 * NP], hT_hi[:, tok], hT_lo[:, tok], KT_hi[:], KT_lo[:])\
                    .then_inc(*pe_qkv.done(f"logits{t}"))

            def qk_prob_T(seq):
                pe.wait_ge(*act_qkv.at(seq, "exp1v"))
                pe.wait_ge(*pool_qkv.at(seq, "k1"))
                transposes(qkv_bank, [q_prob[:, t, i, :] for i in range(2) for t in range(NT)])\
                    .then_inc(*pe_qkv.done("qk_prob_T"))

            def qk(seq):
                pe.wait_ge(*act_qkv.at(seq, "qk_prob_T"))
                for i in range(2):
                    last = mm(qkv_bank[:, i * T:(i + 1) * T], qkV[:, i, :], qkT_prob[:, i, :], start=True, stop=True)
                last.then_inc(*pe_qkv.done("qk"))

            def v_prob_T(seq):
                pe.wait_ge(*dve_qkv.at(seq, "qk_lo"))
                transposes(qkv_bank, [q_exp[:, t, 2, :] for t in range(NT)]).then_inc(*pe_qkv.done("v_prob_T"))

            def v(seq):
                pe.wait_ge(*dve_qkv.at(seq, "v_prob_T"))
                for t in range(NT):
                    last = mm(qkv_bank[:, t * C:(t + 1) * C], vT_prob[:, t * P:(t + 1) * P], vV_sb[:],
                              start=True, stop=True)
                last.then_inc(*pe_qkv.done("v"))

            def row_bank_free(seq, use):
                readers = [*[(dve_row, f"max{i}") for i in range(6)], (act_row, "max_T0"),
                           *[(dve_row, f"max{i}") for i in range(6, 12)], (act_row, "max_T1")]
                reader, name = readers[use - 2]
                if use >= 2:
                    pe.wait_ge(*reader.at(seq, name))
                elif seq.has_before(1):
                    pe.wait_ge(*reader.at(seq, name, back=1))

            def row(seq, i):
                if i == 0:
                    pe.wait_ge(stacked, seq.dmas(STACKS))
                if i % 3 == 0:
                    pe.wait_ge(*pool_qkv.at(seq, f"block{i // 3}"))
                row_bank_free(seq, i + i // 6)
                q, k, dst = q_block[seq.parity], k_stack[seq.parity], row_bank[(i + i // 6) % 2]
                j, kind = divmod(i, 3)
                if kind < 2:
                    for n in range(2):
                        h = G * j + 2 * kind + n
                        mm(dst[:, n * T:(n + 1) * T], q[0:ROWS, h, P:T], k[0:ROWS, h % G, :],
                           start=n == 0, stop=False, skip_group_check=True)
                    mm(dst[:].rearrange("p (a b) -> p a b", a=2)[:, :, P:T], ident_bf[:], row_mask[:, 0:2, :],
                       start=False, stop=True, skip_group_check=True).then_inc(*pe_row.done(f"row{i}"))
                else:
                    for n in range(G):
                        mm(dst[:, n * P:(n + 1) * P], q[0:ROWS, G * j + n, 0:P], k[0:ROWS, n, 0:P],
                           start=n == 0, stop=False, skip_group_check=True)
                    mm(dst[:], ident_bf[:], row_mask[:].rearrange("p a b -> p (a b)"),
                       start=False, stop=True, skip_group_check=True).then_inc(*pe_row.done(f"row{i}"))

            def max_T(seq, half):
                pe.wait_ge(*dve_row.at(seq, f"max{6 * half + 5}"))
                for t in range(NT):
                    last = nc.tensor.transpose(row_bank[half][0:H // 2, t * P:(t + 1) * P],
                                               a_nmax[:, t, half * H // 2:(half + 1) * H // 2], ident[:])
                last.then_inc(*pe_row.done(f"max_T{half}"))

            def col(seq, i):
                if i % 6 == 0:
                    pe.wait_ge(max_moved[i // 6], seq.dmas(1))
                if i >= 2:
                    pe.wait_ge(*act_col.at(seq, f"exp{i - 2}"))
                elif seq.has_before(1):
                    pe.wait_ge(*act_col.at(seq, f"exp{i + 10}", back=1))
                k, dst = k_stack[seq.parity], col_bank[i % 2]
                group, kind = divmod(i, 3)
                half, pair = divmod(group, 2)
                q = q_block[seq.parity][0:ROWS + 1, half * H // 2:(half + 1) * H // 2, :]\
                    .rearrange("p (j g) t -> p g j t", g=G)
                if kind < 2:
                    g = 2 * pair + kind
                    mm(dst[:].rearrange("p (a b) -> p a b", a=2), k[0:ROWS + 1, g, 0:P], q[:, g],
                       start=True, stop=False, skip_group_check=True)
                    mm(dst[:].rearrange("p (a b) -> p a b", a=2)[:, :, 0:P], ident_bf[:], col_mask[:, 0:2, :],
                       start=False, stop=True, skip_group_check=True).then_inc(*pe_col.done(f"col{i}"))
                else:
                    for n in range(2):
                        g = 2 * pair + n
                        mm(dst[:, n * T:(n + 1) * T].rearrange("p (a b) -> p a b", a=2), k[0:ROWS + 1, g, P:T],
                           q[:, g, :, P:T], start=n == 0, stop=False, skip_group_check=True)
                    mm(dst[:], ident_bf[:], col_mask[:].rearrange("p a b -> p (a b)"),
                       start=False, stop=True, skip_group_check=True).then_inc(*pe_col.done(f"col{i}"))

            def pv(seq, j):
                if j == 0:
                    pe.wait_ge(*dve_qkv.at(seq, "v1"))
                    if not seq.has_before(1):
                        pe.wait_ge(act_prep, 5)
                pe.wait_ge(*act_col.at(seq, f"exp{3 * j + 2}"))
                half, pair = divmod(j, 2)
                v_rows = v_head[seq.parity][:].rearrange("p t h r -> p t (h r)")

                def product(n, t, start, stop):
                    at = 32 * (2 * G * half + 2 * n + pair) - 16 * pair
                    probs = (probs0, probs1)[t][j % 2][:, n, :]
                    return mm(pv_bank[32 * n:32 * n + 32, half * T + t * P:(half + 1) * T],
                              v_rows[:, t, at:at + 32], probs, start=start, stop=stop, skip_group_check=True)

                for n in range(G):
                    product(n, 0, start=pair == 0, stop=False)
                for n in range(G):
                    last = product(n, 1, start=False, stop=pair == 1)
                last.then_inc(*pe_col.done(f"pv{j}"))

            def att_T(seq):
                pe.wait_ge(*act_col.at(seq, "out1"))
                if seq.has_before(1):
                    pe.wait_ge(*dve_proj.at(seq, "y1", back=1))
                transposes(pf_bank, [oT_raw[seq.parity][:, half, t * P:(t + 1) * P]
                                     for t in range(NT) for half in range(2)]).then_inc(*pe_proj.done("att_T"))

            def z_T(seq, proj):
                pe.wait_ge(*dve_mix.at(seq, "z1"))
                if proj:
                    pe.wait_ge(*dve_proj.at(proj, "o"))
                else:
                    pe.wait_ge(*dve_proj.at(Sequence(B - 1, 1), "y1"))
                    pe.wait_ge(*dve_ffn.at(seq, "u", back=1))
                transposes(pf_bank, [z_ln[:, t, :] for t in range(NT)]).then_inc(*pe_ffn.done("z_T"))

            def o_T(seq, ffn):
                pe.wait_ge(*dve_proj.at(seq, "o"))
                if ffn:
                    pe.wait_ge(*dve_ffn.at(ffn, "zT_lo"))
                transposes(pf_bank, [o_ln[:, t, :] for t in range(NT)]).then_inc(*pe_proj.done("o_T"))

            def up(seq, half, proj):
                if half == 0:
                    pe.wait_ge(*dve_ffn.at(seq, "zT_lo"))
                if proj:
                    if half == 0:
                        pe.wait_ge(*act_proj.at(proj, "o_T"))
                    else:
                        pe.wait_ge(*act_proj.at(proj, "exp1"))
                elif half == 1:
                    pe.wait_ge(*act_ffn.at(seq, "relu1"))
                for i in range(2):
                    w = W1T[:, (2 * half + i) * P:(2 * half + i + 1) * P]
                    mm(pf_bank[:, i * T:(i + 1) * T], w, zT_hi[:], start=True, stop=False)
                    last = mm(pf_bank[:, i * T:(i + 1) * T], w, zT_lo[:], start=False, stop=True)
                last.then_inc(*pe_ffn.done(f"up{half}"))

            def proj_logits(seq, ffn):
                pe.wait_ge(*act_proj.at(seq, "o_T"))
                if ffn:
                    pe.wait_ge(*act_ffn.at(ffn, "relu1"))
                for t in range(NT):
                    last = mm(pf_bank[:, t * NP:(t + 1) * NP], oT[:, t * P:(t + 1) * P], pKT[:],
                              start=True, stop=True)
                last.then_inc(*pe_proj.done("logits"))

            def proj_prob_T(seq, ffn):
                pe.wait_ge(*act_proj.at(seq, "exp1"))
                if ffn:
                    pe.wait_ge(*act_ffn.at(ffn, "relu3"))
                transposes(pf_bank, [p_exp[:, t, :] for t in range(NT)]).then_inc(*pe_proj.done("prob_T"))

            def down(seq, proj):
                pe.wait_ge(*pool_ffn.at(seq, "lo1"))
                if proj:
                    pe.wait_ge(*dve_proj.at(proj, "prob_T"))
                for part, hid in enumerate((hidden_hi, hidden_lo)):
                    for a in range(FC):
                        last = mm(pf_bank[:, 0:T], W2T[:, a, :], hid[:, a, :],
                                  start=a + part == 0, stop=a == FC - 1 and part == 1)
                last.then_inc(*pe_ffn.done("down"))

            def u_T(seq, mix):
                pe.wait_ge(*dve_ffn.at(seq, "u"))
                pe.wait_ge(*dve_mix.at(mix or Sequence(B - 1, 1), "y1"))
                transposes(mix_bank, [uT[:, t * P:(t + 1) * P] for t in range(NT)]).then_inc(*pe_ffn.done("u_T"))

            def proj_out(seq, ffn):
                pe.wait_ge(*dve_proj.at(seq, "prob_T"))
                if ffn:
                    pe.wait_ge(*dve_ffn.at(ffn, "u"))
                for t in range(NT):
                    last = mm(pf_bank[:, t * C:(t + 1) * C], pT_exp[:, t * P:(t + 1) * P], pV_sb[:],
                              start=True, stop=True)
                last.then_inc(*pe_proj.done("out"))

            def mix_ln_T(seq):
                pe.wait_ge(*dve_proj.at(seq, "ln1"))
                if seq.has_before(1):
                    pe.wait_ge(*dve_mix.at(seq, "y1", back=1))
                if seq.has_before(2):
                    pe.wait_ge(*dve_ffn.at(seq, "ln1", back=2))
                transposes(mix_bank, [f_ln[:, t, :] for t in range(NT)]).then_inc(*pe_mix.done("ln_T"))

            def mix_logits(seq, t):
                if t == 0:
                    pe.wait_ge(*dve_mix.at(seq, "lnT_lo"))
                else:
                    pe.wait_ge(*act_mix.at(seq, "exp0"))
                tok = slice(t * P, (t + 1) * P)
                three_products(mix_bank[:], fT_hi[:, tok], fT_lo[:, tok], fKT_hi[:], fKT_lo[:])\
                    .then_inc(*pe_mix.done(f"logits{t}"))

            def mix_prob_T(seq, t):
                pe.wait_ge(*(act_mix.at(seq, "exp1") if t == 0 else act_mix.at(seq, "prob_T0")))
                transposes(mix_bank, [m_exp[:, t, a * P:(a + 1) * P] for a in range(KC)])\
                    .then_inc(*pe_mix.done(f"prob_T{t}"))

            def mix_out(seq):
                pe.wait_ge(*act_mix.at(seq, "prob_T1"))
                for t in range(NT):
                    for a in range(KC):
                        last = mm(mix_bank[:, t * C:(t + 1) * C], mT_exp[:, t, a, :], fV_sb[:, a, :],
                                  start=a == 0, stop=a == KC - 1)
                last.then_inc(*pe_mix.done("out"))

            def step(qkv, attn, proj, mix, ffn):
                in_order([
                    (col, proj, 9), (mix_ln_T, mix), (col, proj, 10), (pv, proj, 2), (col, proj, 11),
                    (mix_logits, mix, 0), (pv, proj, 3), (row, attn, 0), (att_T, proj), (row, attn, 1),
                    (row, attn, 2), (z_T, ffn, proj), (mix_logits, mix, 1), (row, attn, 3), (o_T, proj, ffn),
                    (row, attn, 4), (qkv_ln_T, qkv), (up, ffn, 0, proj), (row, attn, 5), (mix_prob_T, mix, 0),
                    (qkv_logits, qkv, 0), (max_T, attn, 0), (row, attn, 6), (proj_logits, proj, ffn),
                    (mix_prob_T, mix, 1), (row, attn, 7), (row, attn, 8), (qkv_logits, qkv, 1), (row, attn, 9),
                    (up, ffn, 1, proj), (mix_out, mix), (row, attn, 10), (col, attn, 0), (row, attn, 11),
                    (proj_prob_T, proj, ffn), (qk_prob_T, qkv), (col, attn, 1), (col, attn, 2), (down, ffn, proj),
                    (max_T, attn, 1), (qk, qkv), (u_T, ffn, mix), (proj_out, proj, ffn), (col, attn, 3),
                    (col, attn, 4), (pv, attn, 0), (col, attn, 5), (v_prob_T, qkv), (col, attn, 6), (col, attn, 7),
                    (pv, attn, 1), (col, attn, 8), (v, qkv)])

            run_steps(pe, step, prep_rest)


_INS = ["L0_attn_x", "L0_attn_qK", "L0_attn_qV", "L0_attn_kK", "L0_attn_kV", "L0_attn_vK", "L0_attn_vV",
        "L0_attn_pK", "L0_attn_pV", "L0_attn_fK", "L0_attn_fV", "L0_ffn_W1", "L0_ffn_b1", "L0_ffn_W2", "L0_ffn_b2"]


def kernel(**inputs):
    import numpy as _np
    import concourse.bacc as _bacc
    from concourse import mybir as _mybir
    from concourse.bass_utils import run_bass_kernel_spmd as _run

    nc = _bacc.Bacc("TRN2", target_bir_lowering=False, num_devices=1)
    arrays, args = {}, []
    for name in _INS:
        a = _np.ascontiguousarray(inputs[name])
        arrays[f"in_{name}"] = a
        args.append(nc.dram_tensor(f"in_{name}", a.shape, _mybir.dt.from_np(a.dtype), kind="ExternalInput").ap())
    shape = inputs["L0_attn_x"].shape
    out = nc.dram_tensor("out", shape, _mybir.dt.float32, kind="ExternalOutput").ap()
    build_block(nc, *args, out)
    r = _run(nc, [arrays], core_ids=[0])
    return r.results[0]["out"]
```
